# Optimizing a Trainium2 kernel written in Bass

```python
import numpy as np
import jax
import jax.numpy as jnp

def _softmax(x, axis=-1):
    return jax.nn.softmax(x, axis=axis)

def _gelu(x):
    return jax.nn.gelu(x, approximate=True)

def _silu(x):
    return jax.nn.silu(x)

def _sigmoid(x):
    return jax.nn.sigmoid(x)

def _layernorm(x, axis=-1, eps=1e-05):
    m = jnp.mean(x, axis=axis, keepdims=True)
    v = jnp.var(x, axis=axis, keepdims=True)
    return (x - m) / jnp.sqrt(v + eps)

def _scatter_add(tgt, idx, src, axis=0):
    return tgt.at[idx].add(src)

def _segment_sum(src, seg, n):
    return jax.ops.segment_sum(src, seg, n)
kernel_name = 'mk_gnn_ffn_d1_gnn_r8_22cb78'

def setup_inputs(seed: int=0):
    np.random.seed(seed)
    _w = jnp.asarray

    def _rec_inputs():
        import jax
        import jax.numpy as jnp
        _gk = jax.random.key(seed)
        x = -8.776e-05 + 1 * jax.random.normal(jax.random.fold_in(_gk, 1), (6250, 512), jnp.float32)
        _s = jax.random.randint(jax.random.fold_in(_gk, 2), (50000,), 0, 6250, jnp.int32)
        _d = jax.random.randint(jax.random.fold_in(_gk, 3), (50000,), 0, 6250, jnp.int32)
        _loop = jnp.arange(6250, dtype=jnp.int32)
        src = jnp.concatenate([_s, _d, _loop])
        dst = jnp.concatenate([_d, _s, _loop])
        _o = jnp.argsort(dst, stable=True)
        src = src[_o]
        dst = dst[_o]
        return (x, src, dst)
    x, src, dst = _rec_inputs()

    def _L0_gnn_setup():
        import jax, jax.numpy as jnp
        import numpy as np
        N, E, D, H = (1250, 20000, 512, 8)
        C = D // H
        key = jax.random.key(seed)
        ks = jax.random.split(key, 5)
        x = jax.random.normal(ks[0], (N, D), dtype=jnp.float32)
        edge_index = jax.random.randint(ks[1], (2, E), 0, N, dtype=jnp.int64 if jax.config.jax_enable_x64 else jnp.int32)
        scale = 1.0 / np.sqrt(D).astype(np.float32)
        W_l = jax.random.normal(ks[2], (D, D), dtype=jnp.float32) * scale
        W_r = jax.random.normal(ks[3], (D, D), dtype=jnp.float32) * scale
        att = jax.random.normal(ks[4], (H, C), dtype=jnp.float32) * np.float32(1.0 / np.sqrt(C))
        bias = jnp.zeros((D,), dtype=jnp.float32)
        return {'x': x, 'edge_index': edge_index, 'W_l': W_l, 'W_r': W_r, 'att': att, 'bias': bias}
    _L0_gnn_all = _L0_gnn_setup()
    _L0_gnn_in = {k: v for k, v in _L0_gnn_all.items() if k in ('W_l', 'W_r', 'att', 'bias')}
    del _L0_gnn_all

    def _L0_ffn_setup():
        import jax, jax.numpy as jnp
        import numpy as np
        B, S, D, H, E, K = (2, 256, 512, 256, 16, 2)
        LN_EPS = 1e-05
        key = jax.random.key(seed)
        ks = jax.random.split(key, 9)
        s_in = 1.0 / np.sqrt(D)
        s_hid = 1.0 / np.sqrt(H)
        return {'x': jax.random.normal(ks[0], (B, S, D), dtype=jnp.float32), 'Wg': jax.random.normal(ks[1], (D, E), dtype=jnp.float32) * s_in, 'bg': jax.random.normal(ks[2], (E,), dtype=jnp.float32) * 0.01, 'W1': jax.random.normal(ks[3], (E, D, H), dtype=jnp.float32) * s_in, 'b1': jax.random.normal(ks[4], (E, H), dtype=jnp.float32) * 0.01, 'W2': jax.random.normal(ks[5], (E, H, D), dtype=jnp.float32) * s_hid, 'b2': jax.random.normal(ks[6], (E, D), dtype=jnp.float32) * 0.01, 'gamma': jnp.ones((D,), dtype=jnp.float32), 'beta': jnp.zeros((D,), dtype=jnp.float32)}
    _L0_ffn_all = _L0_ffn_setup()
    _L0_ffn_in = {k: v for k, v in _L0_ffn_all.items() if k in ('Wg', 'bg', 'W1', 'b1', 'W2', 'b2', 'gamma', 'beta')}
    del _L0_ffn_all
    return {'x': x, 'src': src, 'dst': dst, 'L0_gnn_W_l': _L0_gnn_in['W_l'], 'L0_gnn_W_r': _L0_gnn_in['W_r'], 'L0_gnn_att': _L0_gnn_in['att'], 'L0_gnn_bias': _L0_gnn_in['bias'], 'L0_ffn_Wg': _L0_ffn_in['Wg'], 'L0_ffn_bg': _L0_ffn_in['bg'], 'L0_ffn_W1': _L0_ffn_in['W1'], 'L0_ffn_b1': _L0_ffn_in['b1'], 'L0_ffn_W2': _L0_ffn_in['W2'], 'L0_ffn_b2': _L0_ffn_in['b2'], 'L0_ffn_gamma': _L0_ffn_in['gamma'], 'L0_ffn_beta': _L0_ffn_in['beta']}

def reference(x, src, dst, L0_gnn_W_l, L0_gnn_W_r, L0_gnn_att, L0_gnn_bias, L0_ffn_Wg, L0_ffn_bg, L0_ffn_W1, L0_ffn_b1, L0_ffn_W2, L0_ffn_b2, L0_ffn_gamma, L0_ffn_beta):
    import jax
    import jax.numpy as jnp

    def _L0_gnn_ref(x, edge_index, W_l, W_r, att, bias):
        import jax, jax.numpy as jnp
        import numpy as np
        N, E, D, H = (1250, 20000, 512, 8)
        C = D // H
        n = x.shape[0]
        self_idx = jnp.arange(n, dtype=edge_index.dtype)
        src = jnp.concatenate([edge_index[0], self_idx])
        dst = jnp.concatenate([edge_index[1], self_idx])
        x_l = (x @ W_l).reshape(n, H, C)
        x_r = (x @ W_r).reshape(n, H, C)
        m = jax.nn.leaky_relu(x_l[src] + x_r[dst], negative_slope=0.2)
        alpha = jnp.einsum('ehc,hc->eh', m, att)
        amax = jax.lax.stop_gradient(jax.ops.segment_max(alpha, dst, num_segments=n))
        ea = jnp.exp(alpha - amax[dst])
        denom = jax.ops.segment_sum(ea, dst, num_segments=n)
        w = ea / jnp.maximum(denom[dst], 1e-16)
        out = jax.ops.segment_sum(w[:, :, None] * x_l[src], dst, num_segments=n)
        out = out.reshape(n, H * C) + bias
        return jax.nn.elu(out) + x

    def _L0_ffn_ref(x, Wg, bg, W1, b1, W2, b2, gamma, beta):
        import jax, jax.numpy as jnp
        import numpy as np
        B, S, D, H, E, K = (2, 256, 512, 256, 16, 2)
        LN_EPS = 1e-05
        logits = jnp.einsum('bsd,de->bse', x, Wg) + bg
        probs = jax.nn.softmax(logits, axis=-1)
        topk_vals, topk_idx = jax.lax.top_k(probs, K)
        sparse = (jax.nn.one_hot(topk_idx, E, dtype=probs.dtype) * topk_vals[..., None]).sum(axis=-2)
        h = jax.nn.relu(jnp.einsum('bsd,edh->ebsh', x, W1) + b1[:, None, None, :])
        ex = jnp.einsum('ebsh,ehd->ebsd', h, W2) + b2[:, None, None, :]
        out = jnp.einsum('bse,ebsd->bsd', sparse, ex) + x
        mu = out.mean(axis=-1, keepdims=True)
        var = ((out - mu) ** 2).mean(axis=-1, keepdims=True)
        out = (out - mu) * jax.lax.rsqrt(var + LN_EPS) * gamma + beta
        return out
    edge_index = jnp.stack([src, dst])
    x = x + _L0_gnn_ref(_layernorm(x, axis=-1), edge_index, L0_gnn_W_l, L0_gnn_W_r, L0_gnn_att, L0_gnn_bias)
    x = x + _L0_ffn_ref(_layernorm(x, axis=-1)[None], L0_ffn_Wg, L0_ffn_bg, L0_ffn_W1, L0_ffn_b1, L0_ffn_W2, L0_ffn_b2, L0_ffn_gamma, L0_ffn_beta)[0]
    return x

_drawn_inputs = setup_inputs


def setup_inputs(seed=0):
    import zlib

    import numpy as np

    out = dict(_drawn_inputs(seed))
    spreads = {'L0_gnn_bias': (0.0, 0.1), 'L0_ffn_gamma': (1.0, 0.2), 'L0_ffn_beta': (0.0, 0.1)}
    factors = {'L0_ffn_bg': 32.252, 'L0_ffn_b1': 64.0, 'L0_ffn_b2': 55.702}
    for name, (base, spread) in spreads.items():
        noise = np.random.default_rng([zlib.crc32(name.encode()), seed]).standard_normal(out[name].shape)
        drawn = base * np.exp(spread * noise) if base else spread * noise
        out[name] = jnp.asarray(drawn.astype(out[name].dtype))
    for name, factor in factors.items():
        out[name] = (out[name] * factor).astype(out[name].dtype)
    return out
```

```python
from contextlib import ExitStack

import concourse.bass as bass
from concourse import mybir

F32 = mybir.dt.float32
I32 = mybir.dt.int32
U32 = mybir.dt.uint32
BF16 = mybir.dt.bfloat16
ALU = mybir.AluOpType
ACT = mybir.ActivationFunctionType
AX = mybir.AxisListType

P = 128
D = 512
KD = D // P
H = 8
C = D // H
N = 6250
NT = -(-N // P)
NP = NT * P
E = 106250
WPT = -(-E // (P * NT))
EC = WPT * NT
EP = EC * P
EDGES = 24
SLOTS = EDGES + 1
GB = [0, 9, 13, 15, 17, 19, 21, SLOTS]
NG = len(GB) - 1
BINS = 64
UC = -(-(NT + E // EDGES + 2) // P)
ROW = D + H
SLOPE = 0.2
EPS = 1e-5
NEG = 1.0e30
ROUND = 8388608.0
X = 16
HID = 256
KH = HID // P
TILES = (2 * NP + X * (P - 1)) // P


class Mem:

    def __init__(self, nc, stack, stage=""):
        self.nc, self.stack, self.stage, self.sems = nc, stack, stage, []

    def sb(self, name, shape, dt=F32):
        return self.stack.enter_context(self.nc.sbuf_tensor(f"{self.stage}_{name}", shape, dt))

    def ps(self, name, shape=(P, 512)):
        return self.stack.enter_context(self.nc.psum_tensor(f"{self.stage}_{name}", list(shape), F32))

    def sem(self, name):
        s = self.nc.alloc_semaphore(name)
        self.sems.append(s)
        return s

    def give_back(self):
        self.nc.clear_and_free_semaphores(self.sems)
        self.nc.all_engine_barrier()


class Chain:

    def __init__(self, eng, sem):
        self.eng, self.sem, self.n = eng, sem, 0

    def __call__(self, ins):
        self.n += 1
        ins.then_inc(self.sem, 1)
        self.eng.wait_ge(self.sem, self.n)


def after(eng, sem, n):
    if not isinstance(n, int) or n > 0:
        eng.wait_ge(sem, n)


def row_bcast(ap, n):
    return ap.rearrange("(a n) -> a n", a=1).to_broadcast([P, n])


def constants(nc, m):
    k = {}
    k["ident"] = m.sb("ident", [P, P])
    k["upper"] = m.sb("upper", [P, P])
    k["ones"] = m.sb("ones", [P, P])
    k["upper16"] = m.sb("upper16", [P, P], BF16)
    k["ones16"] = m.sb("ones16", [P, P], BF16)
    k["eps"] = m.sb("eps", [P, 1])
    return k


def stage1(nc, k, keep, dram, ins):
    x, src, dst, W_l, W_r, att = (ins[n] for n in ("x", "src", "dst", "W_l", "W_r", "att"))
    ctx = ExitStack()
    with ctx:
        m = Mem(nc, ctx, "s1")
        Wl = m.sb("Wl", [P, KD, D])
        Wr = m.sb("Wr", [P, KD, D])
        Wa = m.sb("Wa", [P, KD, 2 * H])
        tmpW = m.sb("tmpW", [P, KD, D])
        xt = m.sb("xt", [P, 2, D])
        xh = m.sb("xh", [P, 2, D])
        xhT = m.sb("xhT", [P, 2, KD, P])
        stats = m.sb("stats", [P, 2, 6])
        mv = m.sb("mv", [P, 2, 2])
        sd = m.sb("sd", [P, 2])
        rstd = m.sb("rstd", [P, 2])
        rowL = m.sb("rowL", [P, 2, ROW])
        rowR = m.sb("rowR", [P, 2, 2 * D + H])
        dsti = m.sb("dsti", [P, EC], I32)
        parti = m.sb("parti", [P, EC], I32)
        lo = m.sb("lo", [P, EC])
        hi = m.sb("hi", [P, EC])
        iota = m.sb("iota", [P, P])
        ohlo = m.sb("ohlo", [P, 2, WPT, P], BF16)
        ohhi = m.sb("ohhi", [P, 2, WPT, NT], BF16)
        psT = m.ps("psT", (P, 2, 512))
        psL = m.ps("psL", (P, 2, 512))
        psR = m.ps("psR", (P, 2, 512))
        psA = m.ps("psA")
        psC = keep["psC"]

        s_w = m.sem("s1_weights_loaded")
        s_att = m.sem("s1_att_loaded")
        s_dst = m.sem("s1_dst_loaded")
        s_x = [m.sem(f"s1_x_loaded{i}") for i in range(2)]
        s_k = m.sem("s1_constants")
        s_wa = m.sem("s1_score_weights")
        s_part = m.sem("s1_dst_parts")
        s_zero = m.sem("s1_zero_lhs")
        s_bn = m.sem("s1_stats")
        s_mv = m.sem("s1_mean_var")
        s_sd = m.sem("s1_std")
        s_rs = m.sem("s1_rstd")
        s_xh = m.sem("s1_normed")
        s_base = m.sem("s1_base")
        s_T = m.sem("s1_transposed")
        s_Tc = m.sem("s1_transposed_copied")
        s_L = m.sem("s1_left_product")
        s_R = m.sem("s1_right_product")
        s_Lc = m.sem("s1_left_copied")
        s_Rc = m.sem("s1_right_copied")
        s_Ac = m.sem("s1_linear_copied")
        s_oh = m.sem("s1_onehots")
        s_cnt = m.sem("s1_counted")
        s_outL = [m.sem(f"s1_left_stored{i}") for i in range(2)]
        s_outR = [m.sem(f"s1_right_stored{i}") for i in range(2)]
        ch_v = m.sem("s1_vector_chain")
        ch_g = m.sem("s1_pool_chain")

        xv = x.rearrange("(t p) d -> t p d", p=P)
        rowL_d = dram["rowL"].rearrange("(t p) d -> t p d", p=P)
        rowR_d = dram["rowR"].rearrange("(t p) d -> t p d", p=P)

        def tiles(body):
            def gen(eng):
                with eng.Fori(0, NT // 2) as j:
                    body(eng, j, 0)
                    body(eng, j, 1)
                body(eng, NT // 2, 0)
            return gen

        block = ctx.enter_context(nc.Block())

        @block.sync
        def _(sp):
            sp.dma_start(dsti[:, :], dst.rearrange("(p c) -> p c", p=P)).then_inc(s_dst, 16)
            sp.dma_start(Wl[:, :, :], W_l.rearrange("(k p) n -> p k n", p=P)).then_inc(s_w, 16)
            sp.dma_start(Wr[:, :, :], W_r.rearrange("(k p) n -> p k n", p=P)).then_inc(s_w, 16)

            def body(eng, j, par):
                i = 2 * j + par
                eng.wait_ge(s_Lc, i + 1)
                eng.wait_ge(s_Ac, i + 1)
                eng.dma_start(rowL_d[i, :, :], rowL[:, par, :]).then_inc(s_outL[par], 16)
                eng.wait_ge(s_Rc, i + 1)
                eng.wait_ge(s_base, i + 1)
                eng.dma_start(rowR_d[i, :, :], rowR[:, par, :]).then_inc(s_outR[par], 16)
            tiles(body)(sp)
            for par in range(2):
                sp.wait_ge(s_outL[par], 16 * ((NT + 1 - par) // 2))
                sp.wait_ge(s_outR[par], 16 * ((NT + 1 - par) // 2))

        @block.gpsimd
        def _(g):
            ch = Chain(g, ch_g)
            for name in ("ident", "upper"):
                g.memset(k[name][:, :], 0.0 if name == "ident" else 1.0)
            g.memset(k["eps"][:, :], EPS)
            ch(g.memset(k["ones"][:, :], 1.0))
            g.affine_select(out=k["ident"][:, :], in_=k["ident"][:, :], compare_op=ALU.not_equal, fill=1.0,
                            base=0, pattern=[[-1, P]], channel_multiplier=1)
            ch(g.affine_select(out=k["upper"][:, :], in_=k["upper"][:, :], compare_op=ALU.is_gt, fill=0.0,
                               base=0, pattern=[[1, P]], channel_multiplier=-1))
            g.tensor_copy(k["upper16"][:, :], k["upper"][:, :])
            g.tensor_copy(k["ones16"][:, :], k["ones"][:, :])
            g.iota(iota[:, :], pattern=[[1, P]], base=0, channel_multiplier=0,
                   allow_small_or_imprecise_dtypes=True).then_inc(s_k, 1)

            def body(eng, j, par):
                i = 2 * j + par
                if par == 0 and isinstance(j, int) and j == 0:
                    pass
                eng.dma_start(xt[:, par, :], xv[i, :, :]).then_inc(s_x[par], 16)
            body(g, 0, 0)
            body(g, 0, 1)
            with g.Fori(1, NT // 2) as j:
                for par in range(2):
                    g.wait_ge(s_base, 2 * j + par - 1)
                    body(g, j, par)
            g.wait_ge(s_base, NT - 2)
            body(g, NT // 2, 0)

        @block.vector
        def _(v):
            ch = Chain(v, ch_v)
            v.wait_ge(s_att, 16)
            ch(v.tensor_scalar(keep["att"][:, :], keep["att_in"][:, :], 1.0 - SLOPE, None, ALU.mult))
            v.wait_ge(s_w, 32)
            for s, W in enumerate((Wl, Wr)):
                ch(v.tensor_tensor(tmpW[:, :, :], W[:, :, :],
                                   keep["att_in"][:, :].unsqueeze(1).to_broadcast([P, KD, D]), ALU.mult))
                ch(v.tensor_reduce(Wa[:, :, s * H:(s + 1) * H],
                                   tmpW[:, :, :].rearrange("p k (h c) -> p k h c", c=C), AX.X, ALU.add))
            v.tensor_scalar(Wa[:, :, :], Wa[:, :, :], SLOPE, None, ALU.mult).then_inc(s_wa, 1)
            v.wait_ge(s_dst, 16)
            ch(v.tensor_scalar(parti[:, :], dsti[:, :], P - 1, None, ALU.bitwise_and))
            ch(v.tensor_copy(lo[:, :], parti[:, :]))
            ch(v.tensor_scalar(parti[:, :], dsti[:, :], 7, None, ALU.arith_shift_right))
            v.tensor_copy(hi[:, :], parti[:, :]).then_inc(s_part, 1)
            v.wait_ge(s_part, 1)
            v.wait_ge(s_k, 1)

            def body(eng, j, par):
                i = 2 * j + par
                first = isinstance(j, int) and j == 0
                eng.wait_ge(s_x[par], 16 * (j + 1))
                eng.bn_stats(stats[:, par, :], xt[:, par, :]).then_inc(s_bn, 1)
                if not first:
                    eng.wait_ge(s_cnt, i - 1)
                eng.wait_ge(s_bn, i + 1)
                eng.tensor_tensor(ohhi[:, par, :, :],
                                  iota[:, 0:NT].unsqueeze(1).to_broadcast([P, WPT, NT]),
                                  hi[:, bass.ds(i * WPT, WPT)].unsqueeze(2).to_broadcast([P, WPT, NT]),
                                  ALU.is_equal)
                eng.bn_aggr(mv[:, par, :], stats[:, par, :]).then_inc(s_mv, 1)
                eng.tensor_tensor(ohlo[:, par, :, :],
                                  iota[:, :].unsqueeze(1).to_broadcast([P, WPT, P]),
                                  lo[:, bass.ds(i * WPT, WPT)].unsqueeze(2).to_broadcast([P, WPT, P]),
                                  ALU.is_equal).then_inc(s_oh, 1)
                eng.wait_ge(s_sd, i + 1)
                eng.reciprocal(rstd[:, par:par + 1], sd[:, par:par + 1]).then_inc(s_rs, 1)
                eng.wait_ge(s_rs, i + 1)
                if not first:
                    eng.wait_ge(s_T, i - 1)
                eng.tensor_scalar(xh[:, par, :], xt[:, par, :], mv[:, par, 0:1], rstd[:, par:par + 1],
                                  ALU.subtract, ALU.mult).then_inc(s_xh, 1)
                eng.wait_ge(s_xh, i + 1)
                if not first:
                    eng.wait_ge(s_outR[par], 16 * j)
                eng.tensor_tensor(rowR[:, par, D:2 * D], xt[:, par, :], xh[:, par, :], ALU.add).then_inc(s_base, 1)

            body(v, 0, 0)
            body(v, 0, 1)
            with v.Fori(1, NT // 2) as j:
                body(v, j, 0)
                body(v, j, 1)
            body(v, NT // 2, 0)

        @block.scalar
        def _(a):
            a.dma_start(keep["att_in"][:, :], row_bcast(att, D)).then_inc(s_att, 16)
            a.wait_ge(s_k, 1)

            def body(eng, j, par):
                i = 2 * j + par
                first = isinstance(j, int) and j == 0
                last = isinstance(j, int) and j > 0
                if first and par == 0:
                    eng.wait_ge(s_mv, 1)
                    eng.activation(sd[:, 0:1], mv[:, 0, 1:2], ACT.Sqrt, bias=k["eps"][:, 0:1]).then_inc(s_sd, 1)
                eng.wait_ge(s_T, i + 1)
                if not first:
                    eng.wait_ge(s_R, i - 1)
                eng.activation(xhT[:, par, :, :].rearrange("p k n -> p (k n)"), psT[:, par, :], ACT.Copy).then_inc(s_Tc, 1)
                if not last:
                    eng.wait_ge(s_mv, i + 2)
                    if not (first and par == 0):
                        eng.wait_ge(s_rs, i)
                    eng.activation(sd[:, 1 - par:2 - par], mv[:, 1 - par, 1:2], ACT.Sqrt,
                                   bias=k["eps"][:, 0:1]).then_inc(s_sd, 1)
                if not first:
                    eng.wait_ge(s_outL[par], 16 * j)
                    eng.wait_ge(s_outR[par], 16 * j)
                eng.wait_ge(s_L, i + 1)
                eng.activation(rowL[:, par, 0:D], psL[:, par, :], ACT.Copy).then_inc(s_Lc, 1)
                eng.wait_ge(s_R, i + 1)
                eng.activation(rowR[:, par, 0:D], psR[:, par, :], ACT.Copy).then_inc(s_Rc, 1)
                eng.activation(rowL[:, par, D:ROW], psA[:, par * 16:par * 16 + H], ACT.Copy)
                eng.activation(rowR[:, par, 2 * D:2 * D + H], psA[:, par * 16 + H:par * 16 + 2 * H], ACT.Copy).then_inc(s_Ac, 1)

            body(a, 0, 0)
            body(a, 0, 1)
            with a.Fori(1, NT // 2) as j:
                body(a, j, 0)
                body(a, j, 1)
            body(a, NT // 2, 0)

        @block.tensor
        def _(t):
            t.wait_ge(s_k, 1)
            t.wait_ge(s_w, 32)

            def body(eng, j, par):
                i = 2 * j + par
                first = isinstance(j, int) and j == 0
                start = first and par == 0
                last = isinstance(j, int) and j > 0
                eng.wait_ge(s_xh, i + 1)
                if not first:
                    eng.wait_ge(s_Tc, i - 1)
                for c in range(KD):
                    ins = eng.transpose(psT[:, par, c * P:(c + 1) * P], xh[:, par, c * P:(c + 1) * P], k["ident"][:, :])
                ins.then_inc(s_T, 1)
                eng.wait_ge(s_oh, i + 1)
                for w in range(WPT):
                    ins = eng.matmul(psC[:, 0:NT], ohlo[:, par, w, :], ohhi[:, par, w, :],
                                     start=start and w == 0, stop=last and w == WPT - 1)
                ins.then_inc(s_cnt, 1)
                eng.wait_ge(s_Tc, i + 1)
                if start:
                    eng.wait_ge(s_wa, 1)
                if not first:
                    eng.wait_ge(s_Lc, i - 1)
                    eng.wait_ge(s_Rc, i - 1)
                    eng.wait_ge(s_Ac, i - 1)
                for c in range(KD):
                    ins = eng.matmul(psL[:, par, :], xhT[:, par, c, :], Wl[:, c, :], start=c == 0, stop=c == KD - 1)
                ins.then_inc(s_L, 1)
                for c in range(KD):
                    eng.matmul(psA[:, par * 16:par * 16 + 2 * H], xhT[:, par, c, :], Wa[:, c, :],
                               start=c == 0, stop=c == KD - 1)
                for c in range(KD):
                    ins = eng.matmul(psR[:, par, :], xhT[:, par, c, :], Wr[:, c, :], start=c == 0, stop=c == KD - 1)
                ins.then_inc(s_R, 1)

            body(t, 0, 0)
            body(t, 0, 1)
            with t.Fori(1, NT // 2) as j:
                body(t, j, 0)
                body(t, j, 1)
            body(t, NT // 2, 0)
    return m


def stage1b(nc, k, keep, dram):
    psC = keep["psC"]
    CH = BINS * NT // 7
    ctx = ExitStack()
    with ctx:
        m = Mem(nc, ctx, "sb")
        deg = m.sb("deg", [P, NT])
        tot = m.sb("tot", [P, NT])
        incl = m.sb("incl", [P, NT])
        first = m.sb("first_edge", [P, NT])
        key = m.sb("key", [P, NT])
        iob = m.sb("iota_bins", [P, BINS])
        M = m.sb("M", [P, BINS, NT], BF16)
        R = m.sb("R", [P, BINS, NT])
        T = m.sb("T", [P, BINS, NT])
        S = m.sb("S", [P, BINS, NT])
        pos = m.sb("pos", [P, NT])
        posi = m.sb("posi", [P, NT], I32)
        node = m.sb("node", [P, NT])
        nrec = m.sb("nrec", [P, NT, 4], I32)
        ordd = m.sb("ordd", [P, NT], I32)
        ordf = m.sb("ordf", [P, NT])
        K = m.sb("K", [P, NT])
        nsup = m.sb("nsup", [P, NT])
        cin = m.sb("cin", [P, NT])
        cex = m.sb("cex", [P, NT])
        nprev = m.sb("nprev", [P, NT])
        dK = m.sb("dK", [P, NT])
        iu = m.sb("iu", [P, UC])
        G1 = m.sb("G1", [P, UC, NT])
        G2 = m.sb("G2", [P, UC, NT])
        ut = m.sb("ut", [P, UC])
        ub = m.sb("ub", [P, UC])
        uk = m.sb("uk", [P, UC])
        un = m.sb("un", [P, UC])
        tmp = m.sb("tmp_u", [P, UC])
        urec = m.sb("urec", [P, UC, 4], I32)
        tu = m.sb("tu", [1, 2])
        tui = m.sb("tui", [1, 2], I32)
        psR = m.ps("psRank", (P, 2, 512))
        psT = m.ps("psTotal", (P, 2, 512))
        psN = m.ps("psNodes")

        ch_v = m.sem("sb_vector_chain")
        s_io = m.sem("sb_iotas")
        s_deg = m.sem("sb_degrees")
        s_pn = m.sem("sb_node_products")
        s_M = m.sem("sb_bin_masks")
        s_rank = m.sem("sb_ranks")
        s_rc = m.sem("sb_ranks_copied")
        s_nrec = m.sem("sb_node_records")
        s_scat = m.sem("sb_order_stored")
        s_ord = m.sem("sb_order_loaded")
        s_ordf = m.sem("sb_order_float")
        s_K = m.sem("sb_tile_maxima")
        s_u = m.sem("sb_unit_table")
        s_ust = m.sem("sb_unit_table_stored")

        block = ctx.enter_context(nc.Block())

        @block.gpsimd
        def _(g):
            g.iota(iob[:, :], pattern=[[1, BINS]], base=0, channel_multiplier=0,
                   allow_small_or_imprecise_dtypes=True).then_inc(s_io, 1)
            g.iota(node[:, :], pattern=[[P, NT]], base=0, channel_multiplier=1,
                   allow_small_or_imprecise_dtypes=True).then_inc(s_io, 1)
            g.iota(iu[:, :], pattern=[[P, UC]], base=0, channel_multiplier=1,
                   allow_small_or_imprecise_dtypes=True).then_inc(s_io, 1)
            g.wait_ge(s_nrec, 1)
            for c in range(NT):
                g.indirect_dma_start(dram["order"], bass.IndirectOffsetOnAxis(ap=posi[:, c:c + 1], axis=0),
                                     nrec[:, c, :], None).then_inc(s_scat, 16)
            g.wait_ge(s_ordf, 1)
            g.partition_all_reduce(K[:, :], ordf[:, :], P, bass.bass_isa.ReduceOp.max).then_inc(s_K, 1)

        @block.sync
        def _(sp):
            sp.wait_ge(s_scat, 16 * NT)
            with nc.allow_non_contiguous_dma(reason="one field of each node record"):
                sp.dma_start(ordd[:, :], dram["order"].rearrange("(t p) f -> p t f", p=P)[:, :, 2]).then_inc(s_ord, 16)
            sp.wait_ge(s_u, 1)
            sp.dma_start(dram["units"].rearrange("(c p) f -> p c f", p=P), urec[:, :, :]).then_inc(s_ust, 16)
            sp.wait_ge(s_ust, 16)

        @block.tensor
        def _(t):
            t.wait_ge(s_deg, 1)
            t.matmul(psN[:, 0:NT], k["upper"][:, :], deg[:, :], start=True, stop=True)
            t.matmul(psN[:, 64:64 + NT], k["ones"][:, :], deg[:, :], start=True, stop=True).then_inc(s_pn, 1)
            t.wait_ge(s_M, 1)
            Mf = M[:, :, :].rearrange("p b c -> p (b c)")
            for n in range(7):
                if n >= 2:
                    t.wait_ge(s_rc, n - 1)
                t.matmul(psR[:, n % 2, 0:CH], k["upper16"][:, :], Mf[:, n * CH:(n + 1) * CH], start=True, stop=True)
                t.matmul(psT[:, n % 2, 0:CH], k["ones16"][:, :], Mf[:, n * CH:(n + 1) * CH],
                         start=True, stop=True).then_inc(s_rank, 1)

        @block.scalar
        def _(a):
            Rf = R[:, :, :].rearrange("p b c -> p (b c)")
            Tf = T[:, :, :].rearrange("p b c -> p (b c)")
            for n in range(7):
                a.wait_ge(s_rank, n + 1)
                a.activation(Rf[:, n * CH:(n + 1) * CH], psR[:, n % 2, 0:CH], ACT.Copy)
                a.activation(Tf[:, n * CH:(n + 1) * CH], psT[:, n % 2, 0:CH], ACT.Copy).then_inc(s_rc, 1)

        @block.vector
        def _(v):
            ch = Chain(v, ch_v)
            v.tensor_copy(deg[:, :], psC[:, 0:NT]).then_inc(s_deg, 1)
            v.wait_ge(s_deg, 1)
            v.wait_ge(s_io, 3)
            ch(v.tensor_scalar(key[:, :], deg[:, :], float(BINS - 1), None, ALU.min))
            v.tensor_tensor(M[:, :, :], key[:, :].unsqueeze(1).to_broadcast([P, BINS, NT]),
                            iob[:, :].unsqueeze(2).to_broadcast([P, BINS, NT]), ALU.is_equal).then_inc(s_M, 1)
            v.wait_ge(s_pn, 1)
            ch(v.tensor_copy(tot[:, :], psN[:, 64:64 + NT]))
            ch(v.tensor_tensor_scan(incl[:, :], tot[:, :], tot[:, :], 0.0, ALU.add, ALU.bypass))
            ch(v.tensor_tensor(incl[:, :], incl[:, :], tot[:, :], ALU.subtract))
            ch(v.tensor_tensor(first[:, :], incl[:, :], psN[:, 0:NT], ALU.add))
            v.memset(nrec[:, :, 3], 0)
            v.tensor_copy(nrec[:, :, 0], node[:, :])
            v.tensor_copy(nrec[:, :, 1], first[:, :])
            ch(v.tensor_copy(nrec[:, :, 2], deg[:, :]))
            v.wait_ge(s_rc, 7)
            flat = lambda a: a[:, :, :].rearrange("p b c -> p (b c)")
            ch(v.tensor_tensor_scan(flat(S), flat(T), flat(T), 0.0, ALU.add, ALU.bypass))
            ch(v.tensor_tensor(flat(S), flat(S), flat(T), ALU.subtract))
            ch(v.tensor_tensor(flat(S), flat(S), flat(R), ALU.add))
            v.wait_ge(s_M, 1)
            ch(v.tensor_tensor(flat(S), flat(S), flat(M), ALU.mult))
            ch(v.tensor_reduce(pos[:, :], S[:, :, :].rearrange("p b c -> p c b"), AX.X, ALU.add))
            v.tensor_copy(posi[:, :], pos[:, :]).then_inc(s_nrec, 1)
            v.wait_ge(s_ord, 16)
            v.tensor_copy(ordf[:, :], ordd[:, :]).then_inc(s_ordf, 1)
            v.wait_ge(s_K, 1)
            ch(v.tensor_scalar(nsup[:, :], K[:, :], EDGES - 0.5, 1.0 / EDGES, ALU.add, ALU.mult))
            ch(v.tensor_scalar(nsup[:, :], nsup[:, :], -0.5, ROUND, ALU.add, ALU.add))
            ch(v.tensor_scalar(nsup[:, :], nsup[:, :], -ROUND, 1.0, ALU.add, ALU.max))
            ch(v.tensor_tensor_scan(cin[:, :], nsup[:, :], nsup[:, :], 0.0, ALU.add, ALU.bypass))
            v.tensor_tensor(cex[:, :], cin[:, :], nsup[:, :], ALU.subtract)
            v.memset(nprev[:, 0:1], 0.0)
            v.tensor_copy(nprev[:, 1:NT], nsup[:, 0:NT - 1])
            v.tensor_copy(dK[:, 0:1], K[:, 0:1])
            ch(v.tensor_tensor(dK[:, 1:NT], K[:, 1:NT], K[:, 0:NT - 1], ALU.subtract))
            u3 = lambda a: a[:, :].unsqueeze(1).to_broadcast([P, UC, NT])
            ch(v.tensor_tensor(G1[:, :, :], iu[:, :].unsqueeze(2).to_broadcast([P, UC, NT]), u3(cex), ALU.is_ge))
            ch(v.tensor_reduce(ut[:, :], G1[:, :, :], AX.X, ALU.add))
            ch(v.tensor_tensor(G2[:, :, :], G1[:, :, :], u3(nprev), ALU.mult))
            ch(v.tensor_reduce(ub[:, :], G2[:, :, :], AX.X, ALU.add))
            ch(v.tensor_tensor(G2[:, :, :], G1[:, :, :], u3(dK), ALU.mult))
            ch(v.tensor_reduce(uk[:, :], G2[:, :, :], AX.X, ALU.add))
            ch(v.tensor_tensor(ub[:, :], iu[:, :], ub[:, :], ALU.subtract))
            ch(v.tensor_scalar(ub[:, :], ub[:, :], float(EDGES), None, ALU.mult))
            ch(v.tensor_tensor(uk[:, :], uk[:, :], ub[:, :], ALU.subtract))
            ch(v.memset(un[:, :], float(GB[1])))
            for g in range(1, NG):
                ch(v.tensor_scalar(tmp[:, :], uk[:, :], float(GB[g]), float(GB[g + 1] - GB[g]), ALU.is_ge, ALU.mult))
                ch(v.tensor_tensor(un[:, :], un[:, :], tmp[:, :], ALU.add))
            ch(v.tensor_scalar(ut[:, :], ut[:, :], -1.0, float(P), ALU.add, ALU.mult))
            v.tensor_copy(urec[:, :, 0], ut[:, :])
            v.tensor_copy(urec[:, :, 1], un[:, :])
            v.tensor_copy(urec[:, :, 2], ub[:, :])
            v.memset(urec[:, :, 3], 0).then_inc(s_u, 1)
            ch(v.tensor_scalar(tu[0:1, 0:1], cin[0:1, NT - 1:NT], 1.0, None, ALU.add))
            ch(v.tensor_copy(tui[0:1, 0:1], tu[0:1, 0:1]))
            ch(v.tensor_scalar(keep["pairs"][0:1, 0:1], tui[0:1, 0:1], 1, None, ALU.arith_shift_right))
    return m


def stage2(nc, k, keep, dram, ins):
    src, bias = ins["src"], ins["bias"]
    SRC_LEN = src.shape[1]
    ctx = ExitStack()
    with ctx:
        m = Mem(nc, ctx, "s2")
        G = [m.sb(f"G{i}", [P, SLOTS, ROW]) for i in range(2)]
        Z = m.sb("Z", [P, SLOTS, D])
        xrb = m.sb("xrb", [P, 2, 2 * D + H])
        urec = m.sb("urec", [P, 2, 4], I32)
        nrec = m.sb("nrec", [P, 2, 4], I32)
        rows = m.sb("rows", [1, 2], I32)
        start = m.sb("start", [P, 2], I32)
        runs = m.sb("runs", [P, 2, EDGES], I32)
        score = m.sb("score", [P, SLOTS, H])
        expin = m.sb("expin", [P, SLOTS + 1, H])
        ea = m.sb("ea", [P, SLOTS + 1, H])
        slot = m.sb("slot", [P, SLOTS])
        left = m.sb("left", [P, 1])
        off = m.sb("off", [P, SLOTS])
        again = m.sb("again", [P, 1])
        fresh = m.sb("fresh", [P, 1])
        peak = m.sb("peak", [P, H])
        mx = m.sb("mx", [P, H])
        mold = m.sb("mold", [P, H])
        csum = m.sb("csum", [P, H])
        den = m.sb("den", [P, H])
        rden = m.sb("rden", [P, H])
        acc = m.sb("acc", [P, D])
        o = m.sb("o", [P, D])
        orelu = m.sb("orelu", [P, D])
        oexp = m.sb("oexp", [P, D])
        xn = m.sb("xn", [P, 2, D])
        biasb = m.sb("biasb", [P, D])
        nil = m.sb("nil", [P, 16 * NG])
        zero16 = m.sb("zero16", [P, D], BF16)
        psA = m.ps("psAcc", (P, 2, 512))
        psN = m.ps("psNil")

        s_bias = m.sem("s2_bias_loaded")
        s_init = m.sem("s2_initialised")
        s_gate = m.sem("s2_gate")
        s_slot = m.sem("s2_slot_numbers")
        s_urec = [m.sem(f"s2_unit_record_loaded{i}") for i in range(2)]
        s_nrec = [m.sem(f"s2_node_record_loaded{i}") for i in range(2)]
        s_start = m.sem("s2_run_starts")
        s_runs = [m.sem(f"s2_runs_loaded{i}") for i in range(2)]
        s_rowL = [m.sem(f"s2_left_rows_loaded{i}") for i in range(2)]
        s_rowR = [m.sem(f"s2_right_rows_loaded{i}") for i in range(2)]
        s_z = [m.sem(f"s2_sum_formed_group{g}") for g in range(NG)]
        s_relu = [m.sem(f"s2_relu_group{g}") for g in range(NG)]
        s_att = [m.sem(f"s2_times_att_group{g}") for g in range(NG)]
        s_wt = [m.sem(f"s2_weighted_group{g}") for g in range(NG)]
        s_add = [m.sem(f"s2_added_group{g}") for g in range(NG)]
        s_closed = m.sem("s2_sums_closed")
        s_st = [m.sem(f"s2_statistics_step{n}") for n in range(12)]
        s_expin = m.sem("s2_exponents")
        s_ea = m.sem("s2_exponentials")
        s_den = [m.sem(f"s2_denominator_step{n}") for n in range(4)]
        s_ep = [m.sem(f"s2_result_step{n}") for n in range(4)]
        s_o = m.sem("s2_output_rows")
        s_oe = m.sem("s2_output_exponentials")
        s_xn = m.sem("s2_new_rows")
        s_xnst = [m.sem(f"s2_new_rows_stored{i}") for i in range(2)]
        s_row = m.sem("s2_row_kept")

        def wide(ap, n):
            return ap

        def firm(eng):
            eng.sem_inc(s_gate, 1)

        def units(eng, body):
            pairs = eng.value_load(keep["pairs"][0:1, 0:1], min_val=2, max_val=UC * P // 2)
            body(eng, 0, 0)
            body(eng, 0, 1)
            with eng.Fori(1, pairs) as j:
                body(eng, j, 0)
                body(eng, j, 1)
            return pairs

        def slots_of(eng, par):
            firm(eng)
            return eng.value_load(urec[0:1, par, 1:2], min_val=GB[1], max_val=SLOTS)

        block = ctx.enter_context(nc.Block())

        @block.sync
        def _(sp):
            sp.dma_start(biasb[:, :], row_bcast(bias, D)).then_inc(s_bias, 16)

            def body(eng, j, par):
                i = 2 * j + par
                if not (isinstance(j, int)):
                    eng.wait_ge(s_wt[NG - 1], i - 1)
                    eng.wait_ge(s_add[0], i - 1)
                    eng.wait_ge(s_relu[0], i - 1)
                eng.dma_start(urec[:, par, :], dram["units"][bass.ds(i, 1), :].to_broadcast([P, 4])).then_inc(s_urec[par], 16)
                eng.wait_ge(s_urec[par], 16 * (j + 1))
                firm(eng)
                row = eng.value_load(urec[0:1, par, 0:1], min_val=0, max_val=NP - P)
                eng.dma_start(nrec[:, par, :], dram["order"][bass.ds(row, P), :]).then_inc(s_nrec[par], 16)
            units(sp, body)

        @block.gpsimd
        def _(g_):
            g_.iota(slot[:, :], pattern=[[1, SLOTS]], base=-1, channel_multiplier=0,
                    allow_small_or_imprecise_dtypes=True).then_inc(s_slot, 1)
            g_.wait_ge(s_init, 1)

            def body(eng, j, par):
                i = 2 * j + par
                loop = not isinstance(j, int)
                eng.wait_ge(s_urec[par], 16 * (j + 1))
                eng.wait_ge(s_nrec[par], 16 * (j + 1))
                ns = slots_of(eng, par)
                if loop:
                    eng.wait_ge(s_wt[NG - 1], i - 1)
                firm(eng)
                eng.tensor_scalar(start[:, par:par + 1], nrec[:, par, 1:2], urec[:, par, 2:3], float(SRC_LEN - EDGES),
                                  ALU.add, ALU.min).then_inc(s_start, 1)
                eng.wait_ge(s_start, i + 1)
                firm(eng)
                eng.indirect_dma_start(runs[:, par, :], None, src,
                                       bass.IndirectOffsetOnAxis(ap=start[:, par:par + 1], axis=1)).then_inc(s_runs[par], 16)
                eng.indirect_dma_start(G[par][:, 0, :], None, dram["rowL"],
                                       bass.IndirectOffsetOnAxis(ap=nrec[:, par, 0:1], axis=0)).then_inc(s_rowL[par], 16)
                eng.wait_ge(s_runs[par], 16 * (j + 1))
                firm(eng)

                def gather(lo, hi):
                    for s in range(lo, hi):
                        eng.indirect_dma_start(G[par][:, s, :], None, dram["rowL"],
                                               bass.IndirectOffsetOnAxis(ap=runs[:, par, s - 1:s], axis=0)
                                               ).then_inc(s_rowL[par], 16)
                gather(1, GB[1])
                for g in range(1, NG):
                    with eng.If(ns > GB[g]):
                        gather(GB[g], GB[g + 1])
                if loop:
                    eng.wait_ge(s_xn, i - 1)
                    firm(eng)
                eng.indirect_dma_start(xrb[:, par, :], None, dram["rowR"],
                                       bass.IndirectOffsetOnAxis(ap=nrec[:, par, 0:1], axis=0)).then_inc(s_rowR[par], 16)
            units(g_, body)

        @block.scalar
        def _(a):
            a.wait_ge(s_init, 1)

            def result(eng, i, par):
                eng.wait_ge(s_o, i + 1)
                eng.activation(orelu[:, :], o[:, :], ACT.Relu)
                eng.activation(oexp[:, :], o[:, :], ACT.Exp).then_inc(s_oe, 1)

            def store(eng, i, before, par):
                eng.wait_ge(s_xn, i + 1)
                if before is not None:
                    eng.wait_ge(s_xnst[1 - par], before)
                firm(eng)
                row = eng.value_load(rows[0:1, par:par + 1], min_val=0, max_val=NP - P)
                eng.dma_start(dram["xnew"][bass.ds(row, P), :], xn[:, par, :]).then_inc(s_xnst[par], 16)

            def body(eng, j, par):
                i = 2 * j + par
                begin = isinstance(j, int) and par == 0
                eng.wait_ge(s_urec[par], 16 * (j + 1))
                ns = slots_of(eng, par)
                eng.activation(rows[0:1, par:par + 1], urec[0:1, par, 0:1], ACT.Copy).then_inc(s_row, 1)
                for g in range(NG):
                    def relu():
                        eng.wait_ge(s_z[g], i + 1)
                        zg = Z[:, GB[g]:GB[g + 1], :]
                        eng.activation(zg, zg, ACT.Relu).then_inc(s_relu[g], 1)
                    if g == 0:
                        relu()
                        continue
                    with eng.If(ns > GB[g]):
                        relu()
                    with eng.Else():
                        eng.activation(nil[0:1, (12 + par) * NG + g:(12 + par) * NG + g + 1], nil[0:1, 15 * NG:15 * NG + 1], ACT.Copy).then_inc(s_relu[g], 1)
                if not begin:
                    result(eng, i - 1, 1 - par)
                eng.wait_ge(s_expin, i + 1)
                eng.activation(ea[:, :, :], expin[:, :, :], ACT.Exp).then_inc(s_ea, 1)
                if not begin:
                    eng.wait_ge(s_row, i)
                    before = None if isinstance(j, int) and par else 16 * j
                    store(eng, i - 1, before, 1 - par)
            pairs = units(a, body)
            result(a, 2 * pairs - 1, 1)
            store(a, 2 * pairs - 1, 16 * pairs, 1)
            a.wait_ge(s_xnst[0], 16 * pairs)
            a.wait_ge(s_xnst[1], 16 * pairs)
            firm(a)

        @block.tensor
        def _(t):
            def body(eng, j, par):
                i = 2 * j + par
                eng.wait_ge(s_urec[par], 16 * (j + 1))
                ns = slots_of(eng, par)
                if not isinstance(j, int):
                    eng.wait_ge(s_o, i - 1)
                for g in range(NG):
                    def add():
                        eng.wait_ge(s_wt[g], i + 1)
                        for s in range(GB[g], GB[g + 1]):
                            ins = eng.matmul(psA[:, par, :], k["ident"][:, :], Z[:, s, :], start=s == 0, stop=False)
                        ins.then_inc(s_add[g], 1)
                    if g == 0:
                        add()
                        continue
                    with eng.If(ns > GB[g]):
                        add()
                    with eng.Else():
                        eng.matmul(psN[:, par * NG + g:par * NG + g + 1], k["ones16"][:, :], k["ones16"][:, 0:1], start=True, stop=True).then_inc(s_add[g], 1)
                eng.matmul(psA[:, par, :], k["ones16"][:, :], zero16[:, :], start=False, stop=True).then_inc(s_closed, 1)
            units(t, body)

        @block.vector
        def _(v):
            v.memset(nil[:, :], 0.0)
            v.memset(zero16[:, :], 0.0)
            v.memset(score[:, :, :], 0.0)
            v.memset(mx[:, :], 0.0)
            v.memset(den[:, :], 0.0)
            v.memset(acc[:, :], 0.0)
            for p in range(2):
                v.memset(G[p][:, :, D:ROW], 0.0)
            v.memset(rden[:, :], 0.0).then_inc(s_init, 1)
            v.wait_ge(s_init, 1)
            v.wait_ge(s_slot, 1)
            v.wait_ge(s_bias, 16)
            arrived = [v.alloc_register(f"rows_arrived{p}") for p in range(2)]
            for r in arrived:
                v.reg_mov(r, 0)
            heads = lambda ap: ap.rearrange("p (h c) -> p h c", c=C)
            over = lambda ap: ap.unsqueeze(2).to_broadcast([P, H, C])

            def result1(eng, i, par):
                n = i + 1
                eng.wait_ge(s_closed, n)
                eng.tensor_tensor(heads(acc[:, :]), heads(acc[:, :]), over(ea[:, SLOTS, :]), ALU.mult).then_inc(s_ep[0], 1)
                eng.wait_ge(s_ep[0], n)
                eng.tensor_tensor(acc[:, :], acc[:, :], psA[:, par, :], ALU.add).then_inc(s_ep[1], 1)
                eng.wait_ge(s_ep[1], n)
                eng.tensor_tensor(heads(o[:, :]), heads(acc[:, :]), over(rden[:, :]), ALU.mult).then_inc(s_ep[2], 1)
                eng.wait_ge(s_ep[2], n)
                eng.tensor_tensor(o[:, :], o[:, :], biasb[:, :], ALU.add).then_inc(s_o, 1)

            def result2(eng, i, stores, par):
                n = i + 1
                eng.wait_ge(s_oe, n)
                eng.scalar_tensor_tensor(o[:, :], oexp[:, :], 1.0, orelu[:, :], ALU.min, ALU.add).then_inc(s_ep[3], 1)
                eng.wait_ge(s_ep[3], n)
                if stores is not None:
                    eng.wait_ge(s_xnst[0], stores)
                eng.scalar_tensor_tensor(xn[:, par, :], o[:, :], -1.0, xrb[:, par, D:2 * D], ALU.add, ALU.add).then_inc(s_xn, 1)

            def body(eng, j, par):
                i = 2 * j + par
                n = i + 1
                loop = not isinstance(j, int)
                begin = (not loop) and par == 0
                eng.wait_ge(s_urec[par], 16 * (j + 1))
                eng.wait_ge(s_nrec[par], 16 * (j + 1))
                ns = slots_of(eng, par)
                eng.reg_add(arrived[par], arrived[par], eng.to_reg(ns * 16))
                eng.wait_ge(s_rowL[par], eng.snap(arrived[par]))
                eng.wait_ge(s_rowR[par], 16 * (j + 1))

                def when(g, do, sem, kind):
                    at = (4 * kind + par) * NG + g
                    if g == 0:
                        do()
                        return
                    with eng.If(ns > GB[g]):
                        do()
                    with eng.Else():
                        eng.memset(nil[0:1, at:at + 1], 0.0).then_inc(sem, 1)

                for g in range(NG):
                    def form():
                        w = GB[g + 1] - GB[g]
                        if not begin:
                            eng.wait_ge(s_add[g], i)
                        eng.tensor_tensor(Z[:, GB[g]:GB[g + 1], :], G[par][:, GB[g]:GB[g + 1], 0:D],
                                          xrb[:, par, 0:D].unsqueeze(1).to_broadcast([P, w, D]), ALU.add).then_inc(s_z[g], 1)
                    when(g, form, s_z[g], 0)
                if not begin:
                    result1(eng, i - 1, 1 - par)
                for g in range(NG):
                    if g == 1 and not begin:
                        result2(eng, i - 1, 16 * j if loop else None, 1 - par)
                    def times_att():
                        w = GB[g + 1] - GB[g]
                        zg = Z[:, GB[g]:GB[g + 1], :]
                        eng.wait_ge(s_relu[g], n)
                        eng.tensor_tensor(zg, zg, keep["att"][:, :].unsqueeze(1).to_broadcast([P, w, D]), ALU.mult).then_inc(s_att[g], 1)
                        eng.wait_ge(s_att[g], n)
                        eng.tensor_reduce(score[:, GB[g]:GB[g + 1], :], zg.rearrange("p s (h c) -> p s h c", c=C), AX.X, ALU.add)
                    when(g, times_att, s_att[g], 1)
                st = iter(s_st)

                def step(ins):
                    s = next(st)
                    ins.then_inc(s, 1)
                    eng.wait_ge(s, n)
                eng.tensor_tensor(left[:, :], nrec[:, par, 2:3], urec[:, par, 2:3], ALU.subtract)
                eng.tensor_scalar(again[:, :], urec[:, par, 2:3], 0.0, -NEG, ALU.is_gt, ALU.mult)
                step(eng.tensor_scalar(fresh[:, :], urec[:, par, 2:3], 0.0, -NEG, ALU.is_equal, ALU.mult))
                eng.tensor_scalar(mold[:, :], mx[:, :], fresh[:, 0:1], None, ALU.add)
                step(eng.tensor_scalar(off[:, :], slot[:, :], left[:, 0:1], 1.0, ALU.is_lt, ALU.subtract))
                step(eng.tensor_tensor(score[:, :, :], score[:, :, :], G[par][:, :, D:ROW], ALU.add))
                step(eng.tensor_tensor(score[:, :, :], score[:, :, :],
                                       xrb[:, par, 2 * D:2 * D + H].unsqueeze(1).to_broadcast([P, SLOTS, H]), ALU.add))
                step(eng.scalar_tensor_tensor(score[:, :, :], off[:, :].unsqueeze(2).to_broadcast([P, SLOTS, H]), NEG,
                                              score[:, :, :], ALU.mult, ALU.add))
                step(eng.tensor_scalar(score[:, 0, :], score[:, 0, :], again[:, 0:1], None, ALU.add))
                step(eng.tensor_reduce(peak[:, :], score[:, :, :].rearrange("p s h -> p h s"), AX.X, ALU.max))
                step(eng.tensor_tensor(mx[:, :], mold[:, :], peak[:, :], ALU.max))
                eng.tensor_tensor(expin[:, SLOTS, :], mold[:, :], mx[:, :], ALU.subtract)
                eng.tensor_tensor(expin[:, 0:SLOTS, :], score[:, :, :],
                                  mx[:, :].unsqueeze(1).to_broadcast([P, SLOTS, H]), ALU.subtract).then_inc(s_expin, 1)
                eng.wait_ge(s_ea, n)
                for g in range(NG):
                    def weigh():
                        w = GB[g + 1] - GB[g]
                        eng.tensor_tensor(Z[:, GB[g]:GB[g + 1], :].rearrange("p s (h c) -> p s h c", c=C),
                                          G[par][:, GB[g]:GB[g + 1], 0:D].rearrange("p s (h c) -> p s h c", c=C),
                                          ea[:, GB[g]:GB[g + 1], :].unsqueeze(3).to_broadcast([P, w, H, C]),
                                          ALU.mult).then_inc(s_wt[g], 1)
                    when(g, weigh, s_wt[g], 2)
                dn = iter(s_den)
                eng.tensor_reduce(csum[:, :], ea[:, 0:SLOTS, :].rearrange("p s h -> p h s"), AX.X, ALU.add)
                eng.tensor_tensor(den[:, :], den[:, :], ea[:, SLOTS, :], ALU.mult).then_inc(s_den[0], 1)
                eng.wait_ge(s_den[0], n)
                eng.tensor_tensor(den[:, :], den[:, :], csum[:, :], ALU.add).then_inc(s_den[1], 1)
                eng.wait_ge(s_den[1], n)
                eng.tensor_scalar(rden[:, :], den[:, :], 1e-16, None, ALU.max).then_inc(s_den[2], 1)
                eng.wait_ge(s_den[2], n)
                eng.reciprocal(rden[:, :], rden[:, :]).then_inc(s_den[3], 1)
                eng.wait_ge(s_den[3], n)
            pairs = units(v, body)
            result1(v, 2 * pairs - 1, 1)
            result2(v, 2 * pairs - 1, 16 * pairs, 1)
    return m


def node_tiles(eng, body):
    body(eng, 0, 0)
    body(eng, 0, 1)
    with eng.Fori(1, NT // 2) as j:
        body(eng, j, 0)
        body(eng, j, 1)
    body(eng, NT // 2, 0)


def stage3(nc, k, keep, dram, ins):
    Wg, bg = ins["Wg"], ins["bg"]
    NX = NT * X
    ctx = ExitStack()
    with ctx:
        m = Mem(nc, ctx, "s3")
        Wgs = m.sb("Wg", [P, KD, X])
        bgb = m.sb("bg", [P, X])
        xt = m.sb("xt", [P, 2, D])
        xh = m.sb("xh", [P, 2, D])
        xhT = m.sb("xhT", [P, 2, KD, P])
        stats = m.sb("stats", [P, 2, 6])
        mv = m.sb("mv", [P, 2, 2])
        sd = m.sb("sd", [P, 2])
        rstd = m.sb("rstd", [P, 2])
        lg = m.sb("logits", [P, NT, X])
        pr = m.sb("probs", [P, NT, X])
        M = [m.sb(f"chosen{n}", [P, NT, X]) for n in range(2)]
        tmp = m.sb("tmp", [P, NT, X])
        io = m.sb("iota_x", [P, X])
        back = m.sb("iota_back", [P, X])
        top = m.sb("top", [P, NT])
        both = m.sb("both", [P, X, NT], BF16)
        S = m.sb("S", [P, X, NT])
        R = m.sb("R", [P, X, NT])
        T = m.sb("T", [P, X, NT])
        begin = m.sb("begin", [P, X + 1])
        nt = m.sb("nt", [P, X])
        ntc = m.sb("ntc", [P, X])
        base = m.sb("base", [P, X])
        posf = m.sb("posf", [P, NT])
        rowid = m.sb("rowid", [P, NT], I32)
        tj = m.sb("tj", [P, TILES])
        tc = m.sb("tc", [P, TILES, X])
        te = m.sb("te", [P, TILES])
        zi = m.sb("zi", [P, TILES], I32)
        psT = m.ps("psT", (P, 2, 512))
        psG = m.ps("psG")
        psR = m.ps("psRank", (P, 2, 512))
        psS = m.ps("psTotal", (P, 2, 512))

        s_w = m.sem("s3_router_loaded")
        s_x = [m.sem(f"s3_x_loaded{i}") for i in range(2)]
        s_bn = m.sem("s3_stats")
        s_mv = m.sem("s3_mean_var")
        s_sd = m.sem("s3_std")
        s_rs = m.sem("s3_rstd")
        s_xh = m.sem("s3_normed")
        s_T = m.sem("s3_transposed")
        s_Tc = m.sem("s3_transposed_copied")
        s_G = m.sem("s3_router_product")
        s_lg = m.sem("s3_logits")
        s_h = [m.sem(f"s3_normed_stored{i}") for i in range(2)]
        s_io = m.sem("s3_iotas")
        ch_v = m.sem("s3_vector_chain")
        s_ein = m.sem("s3_exponents")
        s_ex = m.sem("s3_exponentials")
        s_both = m.sem("s3_choices")
        s_rank = m.sem("s3_ranks")
        s_rc = m.sem("s3_ranks_copied")
        s_zi = m.sem("s3_zero_ids")
        s_zst = m.sem("s3_row_ids_cleared")
        s_pos = m.sem("s3_places")
        s_scat = m.sem("s3_row_ids_stored")

        xv = dram["xnew"].rearrange("(t p) d -> t p d", p=P)
        hv = dram["hrow"].rearrange("(t p) d -> t p d", p=P)
        block = ctx.enter_context(nc.Block())

        @block.sync
        def _(sp):
            sp.dma_start(Wgs[:, :, :], Wg.rearrange("(k p) n -> p k n", p=P)).then_inc(s_w, 16)
            sp.dma_start(bgb[:, :], row_bcast(bg, X)).then_inc(s_w, 16)

            def body(eng, j, par):
                i = 2 * j + par
                if not (isinstance(j, int) and j == 0):
                    eng.wait_ge(s_xh, i - 1)
                eng.dma_start(xt[:, par, :], xv[i, :, :]).then_inc(s_x[par], 16)
            node_tiles(sp, body)
            sp.dma_start(keep["W1"][:, :, :], ins["W1"].rearrange("e (k p) n -> p (e k) n", p=P)).then_inc(keep["s_W"], 16)
            sp.dma_start(keep["W2"][:, :, :], ins["W2"].rearrange("e (k p) n -> p (e k) n", p=P)).then_inc(keep["s_W"], 16)

        @block.gpsimd
        def _(g):
            g.iota(io[:, :], pattern=[[1, X]], base=0, channel_multiplier=0, allow_small_or_imprecise_dtypes=True).then_inc(s_io, 1)
            g.iota(back[:, :], pattern=[[-1, X]], base=X, channel_multiplier=0, allow_small_or_imprecise_dtypes=True).then_inc(s_io, 1)
            g.iota(rowid[:, :], pattern=[[P, NT]], base=0, channel_multiplier=1).then_inc(s_io, 1)
            g.iota(tj[:, :], pattern=[[1, TILES]], base=0, channel_multiplier=0, allow_small_or_imprecise_dtypes=True).then_inc(s_io, 1)
            g.memset(zi[:, :], 0).then_inc(s_zi, 1)
            g.wait_ge(s_zi, 1)
            g.dma_start(dram["slots"].rearrange("(p j) a -> p (j a)", p=P), zi[:, :]).then_inc(s_zst, 16)
            g.wait_ge(s_zst, 16)
            g.wait_ge(s_io, 3)
            for n in range(2):
                g.wait_ge(s_pos, n + 1)
                for c in range(NT):
                    g.indirect_dma_start(dram["slots"], bass.IndirectOffsetOnAxis(ap=keep["pos"][n][:, c:c + 1], axis=0),
                                         rowid[:, c:c + 1], None).then_inc(s_scat, 16)
            g.wait_ge(s_scat, 16 * 2 * NT)

        @block.tensor
        def _(t):
            t.wait_ge(s_w, 32)

            def body(eng, j, par):
                i = 2 * j + par
                first = isinstance(j, int) and j == 0
                eng.wait_ge(s_xh, i + 1)
                if not first:
                    eng.wait_ge(s_Tc, i - 1)
                for c in range(KD):
                    ins_ = eng.transpose(psT[:, par, c * P:(c + 1) * P], xh[:, par, c * P:(c + 1) * P], k["ident"][:, :])
                ins_.then_inc(s_T, 1)
                eng.wait_ge(s_Tc, i + 1)
                if not first:
                    eng.wait_ge(s_lg, i - 1)
                for c in range(KD):
                    ins_ = eng.matmul(psG[:, par * X:(par + 1) * X], xhT[:, par, c, :], Wgs[:, c, :], start=c == 0, stop=c == KD - 1)
                ins_.then_inc(s_G, 1)
            node_tiles(t, body)
            t.wait_ge(s_both, 1)
            bf = both[:, :, :].rearrange("p e c -> p (e c)")
            for n in range(2):
                w = slice(n * NX // 2, (n + 1) * NX // 2)
                t.matmul(psR[:, n, 0:NX // 2], k["upper16"][:, :], bf[:, w], start=True, stop=True)
                t.matmul(psS[:, n, 0:NX // 2], k["ones16"][:, :], bf[:, w], start=True, stop=True).then_inc(s_rank, 1)

        @block.scalar
        def _(a):
            def body(eng, j, par):
                i = 2 * j + par
                first = isinstance(j, int) and j == 0
                last = isinstance(j, int) and j > 0
                if first and par == 0:
                    eng.wait_ge(s_mv, 1)
                    eng.activation(sd[:, 0:1], mv[:, 0, 1:2], ACT.Sqrt, bias=k["eps"][:, 0:1]).then_inc(s_sd, 1)
                eng.wait_ge(s_T, i + 1)
                if not first:
                    eng.wait_ge(s_G, i - 1)
                eng.activation(xhT[:, par, :, :].rearrange("p k n -> p (k n)"), psT[:, par, :], ACT.Copy).then_inc(s_Tc, 1)
                if not last:
                    eng.wait_ge(s_mv, i + 2)
                    if not (first and par == 0):
                        eng.wait_ge(s_rs, i)
                    eng.activation(sd[:, 1 - par:2 - par], mv[:, 1 - par, 1:2], ACT.Sqrt,
                                   bias=k["eps"][:, 0:1]).then_inc(s_sd, 1)
                eng.wait_ge(s_xh, i + 1)
                eng.dma_start(hv[i, :, :], xh[:, par, :]).then_inc(s_h[par], 16)
            node_tiles(a, body)
            a.wait_ge(s_ein, 1)
            a.activation(pr[:, :, :], lg[:, :, :], ACT.Exp).then_inc(s_ex, 1)
            Rf, Tf = (z[:, :, :].rearrange("p e c -> p (e c)") for z in (R, T))
            for n in range(2):
                w = slice(n * NX // 2, (n + 1) * NX // 2)
                a.wait_ge(s_rank, n + 1)
                a.activation(Rf[:, w], psR[:, n, 0:NX // 2], ACT.Copy)
                a.activation(Tf[:, w], psS[:, n, 0:NX // 2], ACT.Copy).then_inc(s_rc, 1)
            for par in range(2):
                a.wait_ge(s_h[par], 16 * ((NT + 1 - par) // 2))

        @block.vector
        def _(v):
            v.wait_ge(s_w, 32)

            def body(eng, j, par):
                i = 2 * j + par
                first = isinstance(j, int) and j == 0
                eng.wait_ge(s_x[par], 16 * (j + 1))
                eng.bn_stats(stats[:, par, :], xt[:, par, :]).then_inc(s_bn, 1)
                if not (first and par == 0):
                    eng.wait_ge(s_G, i)
                    eng.tensor_tensor(lg[:, bass.ds(i - 1, 1), :], psG[:, (1 - par) * X:(2 - par) * X].unsqueeze(1),
                                      bgb[:, :].unsqueeze(1), ALU.add).then_inc(s_lg, 1)
                    eng.wait_ge(s_bn, i + 1)
                    eng.tensor_copy(mvnil[:, :], stats[:, par, 0:1])
                else:
                    eng.wait_ge(s_bn, 1)
                eng.bn_aggr(mv[:, par, :], stats[:, par, :]).then_inc(s_mv, 1)
                eng.wait_ge(s_sd, i + 1)
                eng.reciprocal(rstd[:, par:par + 1], sd[:, par:par + 1]).then_inc(s_rs, 1)
                eng.wait_ge(s_rs, i + 1)
                if not first:
                    eng.wait_ge(s_T, i - 1)
                    eng.wait_ge(s_h[par], 16 * j)
                eng.tensor_scalar(xh[:, par, :], xt[:, par, :], mv[:, par, 0:1], rstd[:, par:par + 1],
                                  ALU.subtract, ALU.mult).then_inc(s_xh, 1)
            mvnil = m.sb("mvnil", [P, 1])
            node_tiles(v, body)
            ch = Chain(v, ch_v)
            v.wait_ge(s_G, NT)
            v.tensor_tensor(lg[:, NT - 1:NT, :], psG[:, 0:X].unsqueeze(1), bgb[:, :].unsqueeze(1), ALU.add).then_inc(s_lg, 1)
            v.wait_ge(s_lg, NT)
            v.wait_ge(s_io, 4)
            t3 = lambda a: a[:, :].unsqueeze(2).to_broadcast([P, NT, X])
            x3 = lambda a: a[:, :].unsqueeze(1).to_broadcast([P, NT, X])
            ch(v.tensor_reduce(top[:, :], lg[:, :, :], AX.X, ALU.max))
            v.tensor_tensor(lg[:, :, :], lg[:, :, :], t3(top), ALU.subtract).then_inc(s_ein, 1)
            v.wait_ge(s_ex, 1)
            ch(v.tensor_reduce(top[:, :], pr[:, :, :], AX.X, ALU.add))
            ch(v.reciprocal(top[:, :], top[:, :]))
            ch(v.tensor_tensor(pr[:, :, :], pr[:, :, :], t3(top), ALU.mult))
            for n in range(2):
                gate = keep["gate"][n]
                ch(v.tensor_reduce(gate[:, :], pr[:, :, :], AX.X, ALU.max))
                ch(v.tensor_tensor(tmp[:, :, :], pr[:, :, :], t3(gate), ALU.is_equal))
                ch(v.tensor_tensor(tmp[:, :, :], tmp[:, :, :], x3(back), ALU.mult))
                ch(v.tensor_reduce(top[:, :], tmp[:, :, :], AX.X, ALU.max))
                ch(v.tensor_tensor(M[n][:, :, :], t3(top), x3(back), ALU.is_equal))
                if n == 0:
                    ch(v.scalar_tensor_tensor(pr[:, :, :], M[0][:, :, :], -2.0, pr[:, :, :], ALU.mult, ALU.add))
            v.tensor_tensor(both[:, :, :], M[0][:, :, :].rearrange("p c e -> p e c"),
                            M[1][:, :, :].rearrange("p c e -> p e c"), ALU.add).then_inc(s_both, 1)
            v.wait_ge(s_rc, 2)
            flat = lambda a: a[:, :, :].rearrange("p b c -> p (b c)")
            ch(v.tensor_tensor_scan(flat(S), flat(T), flat(T), 0.0, ALU.add, ALU.bypass))
            v.tensor_copy(begin[:, 1:X + 1], S[:, :, NT - 1])
            ch(v.memset(begin[:, 0:1], 0.0))
            ch(v.tensor_tensor(nt[:, :], begin[:, 1:X + 1], begin[:, 0:X], ALU.subtract))
            ch(v.tensor_scalar(nt[:, :], nt[:, :], float(P - 1), 1.0 / P, ALU.add, ALU.mult))
            ch(v.tensor_scalar(nt[:, :], nt[:, :], -0.498, ROUND, ALU.add, ALU.add))
            ch(v.tensor_scalar(nt[:, :], nt[:, :], -ROUND, None, ALU.add))
            ch(v.tensor_tensor_scan(ntc[:, :], nt[:, :], nt[:, :], 0.0, ALU.add, ALU.bypass))
            ch(v.tensor_tensor(base[:, :], ntc[:, :], nt[:, :], ALU.subtract))
            ch(v.tensor_scalar(base[:, :], base[:, :], float(P), None, ALU.mult))
            ch(v.tensor_tensor(base[:, :], base[:, :], begin[:, 0:X], ALU.subtract))
            ch(v.tensor_tensor(flat(S), flat(S), flat(T), ALU.subtract))
            ch(v.tensor_tensor(flat(S), flat(S), flat(R), ALU.add))
            ch(v.tensor_tensor(S[:, :, :], S[:, :, :], base[:, :].unsqueeze(2).to_broadcast([P, X, NT]), ALU.add))
            for n in range(2):
                ch(v.tensor_tensor(tmp[:, :, :], M[n][:, :, :], S[:, :, :].rearrange("p e c -> p c e"), ALU.mult))
                ch(v.tensor_reduce(posf[:, :], tmp[:, :, :], AX.X, ALU.add))
                v.tensor_copy(keep["pos"][n][:, :], posf[:, :]).then_inc(s_pos, 1)
            ch(v.tensor_tensor(tc[:, :, :], tj[:, :].unsqueeze(2).to_broadcast([P, TILES, X]),
                               ntc[:, :].unsqueeze(1).to_broadcast([P, TILES, X]), ALU.is_ge))
            ch(v.tensor_reduce(te[:, :], tc[:, :, :], AX.X, ALU.add))
            ch(v.tensor_scalar(te[:, :], te[:, :], float(X - 1), None, ALU.min))
            ch(v.tensor_copy(keep["expert"][:, :], te[:, :]))
    return m


def stage4(nc, k, keep, dram, ins):
    W1, W2 = keep["W1"], keep["W2"]
    HT = TILES // 2
    assert TILES % 2 == 1
    ctx = ExitStack()
    with ctx:
        m = Mem(nc, ctx, "s4")
        b1 = m.sb("b1", [P, X * HID])
        b2 = m.sb("b2", [P, X * D])
        tokr = m.sb("tokr", [P, P], I32)
        tokf = m.sb("tokf", [P, P])
        tok = m.sb("tok", [P, TILES], I32)
        ids = m.sb("ids", [P, 2], I32)
        xg = m.sb("xg", [P, 2, D])
        xT = m.sb("xT", [P, 2, KD, P])
        h = m.sb("h", [P, 2, HID])
        hT = m.sb("hT", [P, 2, KH, P])
        y = m.sb("y", [P, 2, D])
        psT = m.ps("psT", (P, 2, 512))
        psH = m.ps("psH", (P, 2, 512))
        psY = m.ps("psY", (P, 2, 512))
        psHT = m.ps("psHT", (P, 2, 512))

        s_bias = m.sem("s4_biases_loaded")
        s_clear = m.sem("s4_ids_cleared")
        s_tok = m.sem("s4_ids_loaded")
        s_tokf = m.sem("s4_ids_float")
        s_tokT = m.sem("s4_ids_transposed")
        s_toki = m.sem("s4_ids")
        s_ids = m.sem("s4_tile_ids")
        s_xg = [m.sem(f"s4_rows_gathered{i}") for i in range(2)]
        s_T = m.sem("s4_transposed")
        s_Tc = m.sem("s4_transposed_copied")
        s_H = m.sem("s4_hidden_product")
        s_h = m.sem("s4_hidden_biased")
        s_HT = m.sem("s4_hidden_transposed")
        s_hT = m.sem("s4_hidden_relu")
        s_Y = m.sem("s4_output_product")
        s_y = m.sem("s4_output_biased")
        s_yst = [m.sem(f"s4_output_stored{i}") for i in range(2)]
        s_gate = m.sem("s4_gate")

        yv = dram["yrow"].rearrange("(t p) d -> t p d", p=P)

        def tiles(eng, body):
            body(eng, 0, 0)
            body(eng, 0, 1)
            with eng.Fori(1, HT) as j:
                body(eng, j, 0)
                body(eng, j, 1)
            body(eng, HT, 0)

        def expert(eng, i):
            eng.sem_inc(s_gate, 1)
            return eng.value_load(keep["expert"][0:1, bass.ds(i, 1)], min_val=0, max_val=X - 1)

        block = ctx.enter_context(nc.Block())

        @block.sync
        def _(sp):
            sp.wait_ge(s_clear, 1)
            sp.dma_start(tokr[0:TILES, :], dram["slots"].rearrange("(j p) a -> j (p a)", p=P)).then_inc(s_tok, 16)
            sp.dma_start(b1[:, :], row_bcast(ins["b1"], X * HID)).then_inc(s_bias, 16)
            sp.dma_start(b2[:, :], row_bcast(ins["b2"], X * D)).then_inc(s_bias, 16)

            def body(eng, j, par):
                i = 2 * j + par
                eng.wait_ge(s_y, i + 1)
                eng.dma_start(yv[i, :, :], y[:, par, :]).then_inc(s_yst[par], 16)
            tiles(sp, body)
            sp.wait_ge(s_yst[0], 16 * (HT + 1))
            sp.wait_ge(s_yst[1], 16 * HT)

        @block.gpsimd
        def _(g):
            g.wait_ge(s_toki, 1)

            def body(eng, j, par):
                i = 2 * j + par
                after(eng, s_T, i - 1)
                eng.tensor_copy(ids[:, par:par + 1], tok[:, bass.ds(i, 1)]).then_inc(s_ids, 1)
                eng.wait_ge(s_ids, i + 1)
                eng.sem_inc(s_gate, 1)
                eng.indirect_dma_start(xg[:, par, :], None, dram["hrow"],
                                       bass.IndirectOffsetOnAxis(ap=ids[:, par:par + 1], axis=0)).then_inc(s_xg[par], 16)
            tiles(g, body)

        @block.tensor
        def _(t):
            t.wait_ge(s_tokf, 1)
            t.transpose(psT[:, 0, 0:P], tokf[:, :], k["ident"][:, :]).then_inc(s_tokT, 1)
            t.wait_ge(s_toki, 1)
            t.wait_ge(keep["s_W"], 32)

            def rows_T(eng, j, par):
                i = 2 * j + par
                eng.wait_ge(s_xg[par], 16 * (j + 1))
                after(eng, s_Tc, i - 1)
                for c in range(KD):
                    ins_ = eng.transpose(psT[:, par, c * P:(c + 1) * P], xg[:, par, c * P:(c + 1) * P], k["ident"][:, :])
                ins_.then_inc(s_T, 1)

            def hidden(eng, i, par):
                eng.wait_ge(s_Tc, i + 1)
                after(eng, s_h, i - 1)
                e = expert(eng, i)
                for c in range(KD):
                    ins_ = eng.matmul(psH[:, par, 0:HID], xT[:, par, c, :], W1[:, bass.ds(e * KD + c, 1), :].rearrange("p a n -> p (a n)"),
                                      start=c == 0, stop=c == KD - 1)
                ins_.then_inc(s_H, 1)

            def hidden_T(eng, i, par):
                eng.wait_ge(s_h, i + 1)
                after(eng, s_hT, i - 1)
                for c in range(KH):
                    ins_ = eng.transpose(psHT[:, par, c * P:(c + 1) * P], h[:, par, c * P:(c + 1) * P], k["ident"][:, :])
                ins_.then_inc(s_HT, 1)

            def output(eng, i, par):
                eng.wait_ge(s_hT, i + 1)
                after(eng, s_y, i - 1)
                e = expert(eng, i)
                for c in range(KH):
                    ins_ = eng.matmul(psY[:, par, :], hT[:, par, c, :], W2[:, bass.ds(e * KH + c, 1), :].rearrange("p a n -> p (a n)"),
                                      start=c == 0, stop=c == KH - 1)
                ins_.then_inc(s_Y, 1)

            def body(eng, j, par):
                i = 2 * j + par
                hidden(eng, i, par)
                if not (isinstance(j, int) and i == TILES - 1):
                    rows_T(eng, j + par, 1 - par)
                if not (isinstance(j, int) and i == 0):
                    output(eng, i - 1, 1 - par)
                hidden_T(eng, i, par)
            rows_T(t, 0, 0)
            tiles(t, body)
            output(t, TILES - 1, (TILES - 1) % 2)

        @block.scalar
        def _(a):
            def copy_T(eng, i, par):
                eng.wait_ge(s_T, i + 1)
                after(eng, s_H, i - 1)
                eng.activation(xT[:, par, :, :].rearrange("p k n -> p (k n)"), psT[:, par, :], ACT.Copy).then_inc(s_Tc, 1)

            def body(eng, j, par):
                i = 2 * j + par
                if not (isinstance(j, int) and i == TILES - 1):
                    copy_T(eng, i + 1, 1 - par)
                eng.wait_ge(s_HT, i + 1)
                after(eng, s_Y, i - 1)
                eng.activation(hT[:, par, :, :].rearrange("p k n -> p (k n)"), psHT[:, par, 0:HID], ACT.Relu).then_inc(s_hT, 1)
            copy_T(a, 0, 0)
            tiles(a, body)

        @block.vector
        def _(v):
            v.memset(tokr[:, :], 0).then_inc(s_clear, 1)
            v.wait_ge(s_tok, 16)
            v.tensor_copy(tokf[:, :], tokr[:, :]).then_inc(s_tokf, 1)
            v.wait_ge(s_tokT, 1)
            v.tensor_copy(tok[:, :], psT[:, 0, 0:TILES]).then_inc(s_toki, 1)
            v.wait_ge(s_bias, 32)

            def output(eng, i, j, par):
                e = expert(eng, i)
                eng.wait_ge(s_Y, i + 1)
                after(eng, s_yst[par], 16 * j)
                eng.tensor_tensor(y[:, par, :], psY[:, par, :], b2[:, bass.ds(e * D, D)], ALU.add).then_inc(s_y, 1)

            def body(eng, j, par):
                i = 2 * j + par
                e = expert(eng, i)
                eng.wait_ge(s_H, i + 1)
                after(eng, s_HT, i - 1)
                eng.tensor_tensor(h[:, par, :], psH[:, par, 0:HID], b1[:, bass.ds(e * HID, HID)], ALU.add).then_inc(s_h, 1)
                if not (isinstance(j, int) and i == 0):
                    output(eng, i - 1, j + par - 1, 1 - par)
            tiles(v, body)
            output(v, TILES - 1, HT, (TILES - 1) % 2)
    return m


def stage5(nc, k, keep, dram, ins):
    B = 4
    assert NT % B == 1
    ctx = ExitStack()
    with ctx:
        m = Mem(nc, ctx, "s5")
        gam = m.sb("gamma", [P, D])
        bet = m.sb("beta", [P, D])
        pc = m.sb("pc", [P, B, 2], I32)
        y1 = m.sb("y1", [P, B, D])
        y2 = m.sb("y2", [P, B, D])
        hr = m.sb("hr", [P, B, D])
        xr = m.sb("xr", [P, B, D])
        nid = m.sb("nid", [P, B, 4], I32)
        a1 = m.sb("a1", [P, B, D])
        a2 = m.sb("a2", [P, B, D])
        xb = m.sb("xb", [P, B, D])
        nrm = m.sb("nrm", [P, B, D])
        res = m.sb("res", [P, B, D])
        stats = m.sb("stats", [P, B, 6])
        mv = m.sb("mv", [P, B, 2])
        sd = m.sb("sd", [P, B])
        rstd = m.sb("rstd", [P, B])

        s_gb = m.sem("s5_gamma_beta_loaded")
        s_in = [m.sem(f"s5_rows_loaded{i}") for i in range(B)]
        s_y = [m.sem(f"s5_choices_gathered{i}") for i in range(B)]
        s_pc = m.sem("s5_places")
        s_a1 = m.sem("s5_first_choice")
        s_a2 = m.sem("s5_both_choices")
        s_bn = m.sem("s5_stats")
        s_mv = m.sem("s5_mean_var")
        s_sd = m.sem("s5_std")
        s_rs = m.sem("s5_rstd")
        s_g = m.sem("s5_centred_times_gamma")
        s_xb = m.sem("s5_residual_plus_beta")
        s_r = m.sem("s5_results")
        s_out = [m.sem(f"s5_results_stored{i}") for i in range(B)]
        s_gate = m.sem("s5_gate")
        tile_of = lambda name, i: dram[name].rearrange("(t p) d -> t p d", p=P)[i, :, :]

        def steps(eng, body):
            for q in range(B):
                body(q, 0, q)
            with eng.Fori(1, NT // B) as j:
                for q in range(B):
                    body(B * j + q, j, q)
            body(NT - 1, NT // B, 0)

        block = ctx.enter_context(nc.Block())

        @block.sync
        def _(sp):
            sp.dma_start(gam[:, :], row_bcast(ins["gamma"], D)).then_inc(s_gb, 16)
            sp.dma_start(bet[:, :], row_bcast(ins["beta"], D)).then_inc(s_gb, 16)

            def body(i, j, q):
                after(sp, s_r, i - B + 1)
                sp.sem_inc(s_gate, 1)
                after(sp, s_out[q], 16 * j)
                sp.dma_start(hr[:, q, :], tile_of("hrow", i)).then_inc(s_in[q], 16)
                sp.dma_start(xr[:, q, :], tile_of("xnew", i)).then_inc(s_in[q], 16)
                sp.dma_start(nid[:, q, :], tile_of("order", i)).then_inc(s_in[q], 16)
            steps(sp, body)

        @block.gpsimd
        def _(g):
            def scatter(i, j, q):
                g.wait_ge(s_r, i + 1)
                g.wait_ge(s_in[q], 48 * (j + 1))
                g.sem_inc(s_gate, 1)
                g.indirect_dma_start(dram["out"], bass.IndirectOffsetOnAxis(ap=nid[:, q, 0:1], axis=0),
                                     res[:, q, :], None).then_inc(s_out[q], 16)

            def body(i, j, q):
                after(g, s_a2, i - B + 1)
                for n in range(2):
                    ins_ = g.tensor_copy(pc[:, q, n:n + 1], keep["pos"][n][:, bass.ds(i, 1)])
                ins_.then_inc(s_pc, 1)
                g.wait_ge(s_pc, i + 1)
                g.sem_inc(s_gate, 1)
                for n, y in enumerate((y1, y2)):
                    g.indirect_dma_start(y[:, q, :], None, dram["yrow"],
                                         bass.IndirectOffsetOnAxis(ap=pc[:, q, n:n + 1], axis=0)).then_inc(s_y[q], 16)
                if not (isinstance(i, int) and i < 2):
                    scatter(i - 2, j if q >= 2 else j - 1, (q - 2) % B)
            steps(g, body)
            scatter(NT - 2, NT // B - 1, B - 1)
            scatter(NT - 1, NT // B, 0)
            for q in range(B):
                g.wait_ge(s_out[q], 16 * (NT // B + (q == 0)))

        @block.scalar
        def _(a):
            def body(i, j, q):
                a.wait_ge(s_mv, i + 1)
                after(a, s_rs, i - B + 1)
                a.activation(sd[:, q:q + 1], mv[:, q, 1:2], ACT.Sqrt, bias=k["eps"][:, 0:1]).then_inc(s_sd, 1)
            steps(a, body)

        @block.vector
        def _(v):
            v.wait_ge(s_gb, 32)

            def body(i, j, q):
                g1, g2 = (keep["gate"][n][:, bass.ds(i, 1)] for n in range(2))
                before = not (isinstance(i, int) and i == 0)
                jp, qp = (j, q - 1) if q else (j - 1, B - 1)
                v.wait_ge(s_y[q], 32 * (j + 1))
                v.wait_ge(s_in[q], 48 * (j + 1))
                v.scalar_tensor_tensor(a1[:, q, :], y1[:, q, :], g1, hr[:, q, :], ALU.mult, ALU.add).then_inc(s_a1, 1)
                if before:
                    v.wait_ge(s_sd, i)
                    v.reciprocal(rstd[:, qp:qp + 1], sd[:, qp:qp + 1]).then_inc(s_rs, 1)
                v.tensor_tensor(xb[:, q, :], xr[:, q, :], bet[:, :], ALU.add).then_inc(s_xb, 1)
                v.wait_ge(s_a1, i + 1)
                v.scalar_tensor_tensor(a2[:, q, :], y2[:, q, :], g2, a1[:, q, :], ALU.mult, ALU.add).then_inc(s_a2, 1)
                if before:
                    centre(i - 1, qp)
                v.wait_ge(s_a2, i + 1)
                v.bn_stats(stats[:, q, :], a2[:, q, :]).then_inc(s_bn, 1)
                if before:
                    result(i - 1, jp, qp)
                v.wait_ge(s_bn, i + 1)
                v.tensor_copy(nil[:, 0:1], stats[:, q, 0:1])
                v.bn_aggr(mv[:, q, :], stats[:, q, :]).then_inc(s_mv, 1)

            def centre(i, q):
                v.wait_ge(s_mv, i + 1)
                v.scalar_tensor_tensor(nrm[:, q, :], a2[:, q, :], mv[:, q, 0:1], gam[:, :], ALU.subtract, ALU.mult).then_inc(s_g, 1)

            def result(i, j, q):
                v.wait_ge(s_g, i + 1)
                v.wait_ge(s_rs, i + 1)
                v.wait_ge(s_xb, i + 1)
                after(v, s_out[q], 16 * j)
                v.scalar_tensor_tensor(res[:, q, :], nrm[:, q, :], rstd[:, q:q + 1], xb[:, q, :], ALU.mult, ALU.add).then_inc(s_r, 1)
            nil = m.sb("nil", [P, 1])
            steps(v, body)
            v.wait_ge(s_sd, NT)
            v.reciprocal(rstd[:, 0:1], sd[:, 0:1]).then_inc(s_rs, 1)
            centre(NT - 1, 0)
            result(NT - 1, NT // B, 0)


def build(nc, a, out):
    dram = {"out": out}
    for name, shape, dt in (("rowL", (NP, ROW), F32), ("rowR", (NP, 2 * D + H), F32), ("order", (NP, 4), I32),
                            ("units", (UC * P, 4), I32), ("xnew", (NP, D), F32), ("hrow", (NP, D), F32),
                            ("slots", (TILES * P, 1), I32), ("yrow", (TILES * P, D), F32)):
        dram[name] = nc.dram_tensor(f"tmp_{name}", shape, dt).ap()
    ctx = ExitStack()
    with ctx:
        m = Mem(nc, ctx, "all")
        k = constants(nc, m)
        keep = {"pairs": m.sb("pairs", [1, 1], I32),
                "pos": [m.sb(f"pos{n}", [P, NT], I32) for n in range(2)],
                "gate": [m.sb(f"gate{n}", [P, NT]) for n in range(2)],
                "expert": m.sb("expert", [P, TILES], I32),
                "s_W": m.sem("expert_weights_loaded")}
        graph = ExitStack()
        with graph:
            g = Mem(nc, graph, "graph")
            keep["att"] = g.sb("att_pos", [P, D])
            keep["att_in"] = g.sb("att_in", [P, D])
            count = ExitStack()
            with count:
                keep["psC"] = Mem(nc, count, "count").ps("psC")
                stage1(nc, k, keep, dram, a).give_back()
                stage1b(nc, k, keep, dram).give_back()
                stage2(nc, k, keep, dram, a).give_back()
        experts = ExitStack()
        with experts:
            x = Mem(nc, experts, "experts")
            keep["W1"] = x.sb("W1", [P, X * KD, HID])
            keep["W2"] = x.sb("W2", [P, X * KH, D])
            stage3(nc, k, keep, dram, a).give_back()
            stage4(nc, k, keep, dram, a).give_back()
        stage5(nc, k, keep, dram, a)


def kernel(x, src, dst, L0_gnn_W_l, L0_gnn_W_r, L0_gnn_att, L0_gnn_bias, L0_ffn_Wg, L0_ffn_bg, L0_ffn_W1,
           L0_ffn_b1, L0_ffn_W2, L0_ffn_b2, L0_ffn_gamma, L0_ffn_beta):
    import concourse.bacc as bacc
    import numpy as np
    from concourse.bass_utils import run_bass_kernel_spmd

    def padded(a, n, fill):
        a = np.asarray(a)
        return np.concatenate([a, np.full((n - a.shape[0],) + a.shape[1:], fill, a.dtype)])

    arrays = {
        "x": padded(x, NP, 0),
        "src": padded(src, E + P, 0).reshape(1, -1),
        "dst": padded(dst, EP, NT * P + P),
        "W_l": L0_gnn_W_l, "W_r": L0_gnn_W_r, "att": np.reshape(L0_gnn_att, -1), "bias": L0_gnn_bias,
        "Wg": L0_ffn_Wg, "bg": L0_ffn_bg, "W1": L0_ffn_W1, "b1": np.reshape(L0_ffn_b1, -1),
        "W2": L0_ffn_W2, "b2": np.reshape(L0_ffn_b2, -1), "gamma": L0_ffn_gamma, "beta": L0_ffn_beta,
    }
    arrays = {f"in_{n}": np.ascontiguousarray(v) for n, v in arrays.items()}
    nc = bacc.Bacc("TRN2", target_bir_lowering=False, num_devices=1)
    a = {n[3:]: nc.dram_tensor(n, v.shape, mybir.dt.from_np(v.dtype), kind="ExternalInput").ap() for n, v in arrays.items()}
    out = nc.dram_tensor("out_rows", (NP, D), F32, kind="ExternalOutput").ap()
    build(nc, a, out)
    r = run_bass_kernel_spmd(nc, [arrays], core_ids=[0])
    return r.results[0]["out_rows"][:N]
```

```python
from contextlib import ExitStack

import concourse.bass as bass
from concourse import mybir

F32 = mybir.dt.float32
I32 = mybir.dt.int32
U32 = mybir.dt.uint32
BF16 = mybir.dt.bfloat16
ALU = mybir.AluOpType
ACT = mybir.ActivationFunctionType
AX = mybir.AxisListType

P = 128
D = 512
KD = D // P
H = 8
C = D // H
N = 6250
NT = -(-N // P)
NP = NT * P
E = 106250
WPT = -(-E // (P * NT))
EC = WPT * NT
EP = EC * P
EDGES = 24
SLOTS = EDGES + 1
GB = [0, 9, 13, 15, 17, 19, 21, SLOTS]
FIX = GB[1]
PEELED = 3
WMAX = max(b - a for a, b in zip(GB[1:], GB[2:]))
NG = len(GB) - 1
BINS = 64
UC = -(-(NT + E // EDGES + 2) // P)
ROW = D + H
SLOPE = 0.2
EPS = 1e-5
NEG = 1.0e30
ROUND = 8388608.0
X = 16
HID = 256
KH = HID // P
TILES = (2 * NP + X * (P - 1)) // P


class Mem:

    def __init__(self, nc, stack, stage=""):
        self.nc, self.stack, self.stage, self.sems = nc, stack, stage, []

    def sb(self, name, shape, dt=F32):
        return self.stack.enter_context(self.nc.sbuf_tensor(f"{self.stage}_{name}", shape, dt))

    def ps(self, name, shape=(P, 512)):
        return self.stack.enter_context(self.nc.psum_tensor(f"{self.stage}_{name}", list(shape), F32))

    def sem(self, name):
        s = self.nc.alloc_semaphore(name)
        self.sems.append(s)
        return s

    def give_back(self):
        self.nc.clear_and_free_semaphores(self.sems)
        self.nc.all_engine_barrier()


class Chain:

    def __init__(self, eng, sem):
        self.eng, self.sem, self.n = eng, sem, 0

    def __call__(self, ins):
        self.n += 1
        ins.then_inc(self.sem, 1)
        self.eng.wait_ge(self.sem, self.n)


def after(eng, sem, n):
    if not isinstance(n, int) or n > 0:
        eng.wait_ge(sem, n)


def row_bcast(ap, n):
    return ap.rearrange("(a n) -> a n", a=1).to_broadcast([P, n])


def constants(nc, m):
    k = {}
    k["ident"] = m.sb("ident", [P, P])
    k["upper"] = m.sb("upper", [P, P])
    k["ones"] = m.sb("ones", [P, P])
    k["upper16"] = m.sb("upper16", [P, P], BF16)
    k["ones16"] = m.sb("ones16", [P, P], BF16)
    k["eps"] = m.sb("eps", [P, 1])
    return k


def stage1(nc, k, keep, dram, ins):
    x, src, dst, W_l, W_r, att = (ins[n] for n in ("x", "src", "dst", "W_l", "W_r", "att"))
    ctx = ExitStack()
    with ctx:
        m = Mem(nc, ctx, "s1")
        Wl = m.sb("Wl", [P, KD, D])
        Wr = m.sb("Wr", [P, KD, D])
        Wa = m.sb("Wa", [P, KD, 2 * H])
        tmpW = m.sb("tmpW", [P, KD, D])
        att_in = m.sb("att_in", [P, D])
        xt = m.sb("xt", [P, 2, D])
        xh = m.sb("xh", [P, 2, D])
        xhT = m.sb("xhT", [P, 2, KD, P])
        stats = m.sb("stats", [P, 2, 6])
        mv = m.sb("mv", [P, 2, 2])
        sd = m.sb("sd", [P, 2])
        rstd = m.sb("rstd", [P, 2])
        rowL = m.sb("rowL", [P, 2, ROW])
        rowR = m.sb("rowR", [P, 2, ROW])
        rowX = m.sb("rowX", [P, 2, D])
        dsti = m.sb("dsti", [P, EC], I32)
        parti = m.sb("parti", [P, EC], I32)
        lo = m.sb("lo", [P, EC])
        hi = m.sb("hi", [P, EC])
        iota = m.sb("iota", [P, P])
        ohlo = m.sb("ohlo", [P, 2, WPT, P], BF16)
        ohhi = m.sb("ohhi", [P, 2, WPT, NT], BF16)
        psT = m.ps("psT", (P, 2, 512))
        psL = m.ps("psL", (P, 2, 512))
        psR = m.ps("psR", (P, 2, 512))
        psA = m.ps("psA")
        psC = keep["psC"]

        s_w = m.sem("s1_weights_loaded")
        s_att = m.sem("s1_att_loaded")
        s_dst = m.sem("s1_dst_loaded")
        s_x = [m.sem(f"s1_x_loaded{i}") for i in range(2)]
        s_k = m.sem("s1_constants")
        s_wa = m.sem("s1_score_weights")
        s_part = m.sem("s1_dst_parts")
        s_zero = m.sem("s1_zero_lhs")
        s_bn = m.sem("s1_stats")
        s_mv = m.sem("s1_mean_var")
        s_sd = m.sem("s1_std")
        s_rs = m.sem("s1_rstd")
        s_xh = m.sem("s1_normed")
        s_base = m.sem("s1_base")
        s_T = m.sem("s1_transposed")
        s_Tc = m.sem("s1_transposed_copied")
        s_L = m.sem("s1_left_product")
        s_R = m.sem("s1_right_product")
        s_Lc = m.sem("s1_left_copied")
        s_Rc = m.sem("s1_right_copied")
        s_Ac = m.sem("s1_linear_copied")
        s_oh = m.sem("s1_onehots")
        s_cnt = m.sem("s1_counted")
        s_outL = [m.sem(f"s1_left_stored{i}") for i in range(2)]
        s_outR = [m.sem(f"s1_right_stored{i}") for i in range(2)]
        ch_v = m.sem("s1_vector_chain")
        ch_g = m.sem("s1_pool_chain")

        xv = x.rearrange("(t p) d -> t p d", p=P)
        rowL_d = dram["rowL"].rearrange("(t p) d -> t p d", p=P)
        rowR_d = dram["rowR"].rearrange("(t p) d -> t p d", p=P)
        rowX_d = dram["rowX"].rearrange("(t p) d -> t p d", p=P)

        def tiles(body):
            def gen(eng):
                with eng.Fori(0, NT // 2) as j:
                    body(eng, j, 0)
                    body(eng, j, 1)
                body(eng, NT // 2, 0)
            return gen

        block = ctx.enter_context(nc.Block())

        @block.sync
        def _(sp):
            sp.dma_start(dsti[:, :], dst.rearrange("(p c) -> p c", p=P)).then_inc(s_dst, 16)
            sp.dma_start(Wl[:, :, :], W_l.rearrange("(k p) n -> p k n", p=P)).then_inc(s_w, 16)
            sp.dma_start(Wr[:, :, :], W_r.rearrange("(k p) n -> p k n", p=P)).then_inc(s_w, 16)

            def body(eng, j, par):
                i = 2 * j + par
                eng.wait_ge(s_Lc, i + 1)
                eng.wait_ge(s_Ac, i + 1)
                eng.dma_start(rowL_d[i, :, :], rowL[:, par, :]).then_inc(s_outL[par], 16)
                eng.wait_ge(s_Rc, i + 1)
                eng.dma_start(rowR_d[i, :, :], rowR[:, par, :]).then_inc(s_outR[par], 16)
                eng.wait_ge(s_base, i + 1)
                eng.dma_start(rowX_d[i, :, :], rowX[:, par, :]).then_inc(s_outR[par], 16)
            tiles(body)(sp)
            for par in range(2):
                sp.wait_ge(s_outL[par], 16 * ((NT + 1 - par) // 2))
                sp.wait_ge(s_outR[par], 32 * ((NT + 1 - par) // 2))

        @block.gpsimd
        def _(g):
            ch = Chain(g, ch_g)
            for name in ("ident", "upper"):
                g.memset(k[name][:, :], 0.0 if name == "ident" else 1.0)
            g.memset(k["eps"][:, :], EPS)
            ch(g.memset(k["ones"][:, :], 1.0))
            g.affine_select(out=k["ident"][:, :], in_=k["ident"][:, :], compare_op=ALU.not_equal, fill=1.0,
                            base=0, pattern=[[-1, P]], channel_multiplier=1)
            ch(g.affine_select(out=k["upper"][:, :], in_=k["upper"][:, :], compare_op=ALU.is_gt, fill=0.0,
                               base=0, pattern=[[1, P]], channel_multiplier=-1))
            g.tensor_copy(k["upper16"][:, :], k["upper"][:, :])
            g.tensor_copy(k["ones16"][:, :], k["ones"][:, :])
            g.iota(iota[:, :], pattern=[[1, P]], base=0, channel_multiplier=0,
                   allow_small_or_imprecise_dtypes=True).then_inc(s_k, 1)

            def body(eng, j, par):
                i = 2 * j + par
                if par == 0 and isinstance(j, int) and j == 0:
                    pass
                eng.dma_start(xt[:, par, :], xv[i, :, :]).then_inc(s_x[par], 16)
            body(g, 0, 0)
            body(g, 0, 1)
            with g.Fori(1, NT // 2) as j:
                for par in range(2):
                    g.wait_ge(s_base, 2 * j + par - 1)
                    body(g, j, par)
            g.wait_ge(s_base, NT - 2)
            body(g, NT // 2, 0)

        @block.vector
        def _(v):
            ch = Chain(v, ch_v)
            v.wait_ge(s_att, 16)
            ch(v.tensor_scalar(keep["att"][:, :], att_in[:, :], 1.0 - SLOPE, None, ALU.mult))
            v.wait_ge(s_w, 32)
            for s, W in enumerate((Wl, Wr)):
                ch(v.tensor_tensor(tmpW[:, :, :], W[:, :, :],
                                   att_in[:, :].unsqueeze(1).to_broadcast([P, KD, D]), ALU.mult))
                ch(v.tensor_reduce(Wa[:, :, s * H:(s + 1) * H],
                                   tmpW[:, :, :].rearrange("p k (h c) -> p k h c", c=C), AX.X, ALU.add))
            v.tensor_scalar(Wa[:, :, :], Wa[:, :, :], SLOPE, None, ALU.mult).then_inc(s_wa, 1)
            v.wait_ge(s_dst, 16)
            ch(v.tensor_scalar(parti[:, :], dsti[:, :], P - 1, None, ALU.bitwise_and))
            ch(v.tensor_copy(lo[:, :], parti[:, :]))
            ch(v.tensor_scalar(parti[:, :], dsti[:, :], 7, None, ALU.arith_shift_right))
            v.tensor_copy(hi[:, :], parti[:, :]).then_inc(s_part, 1)
            v.wait_ge(s_part, 1)
            v.wait_ge(s_k, 1)

            def body(eng, j, par):
                i = 2 * j + par
                first = isinstance(j, int) and j == 0
                eng.wait_ge(s_x[par], 16 * (j + 1))
                eng.bn_stats(stats[:, par, :], xt[:, par, :]).then_inc(s_bn, 1)
                if not first:
                    eng.wait_ge(s_cnt, i - 1)
                eng.wait_ge(s_bn, i + 1)
                eng.tensor_tensor(ohhi[:, par, :, :],
                                  iota[:, 0:NT].unsqueeze(1).to_broadcast([P, WPT, NT]),
                                  hi[:, bass.ds(i * WPT, WPT)].unsqueeze(2).to_broadcast([P, WPT, NT]),
                                  ALU.is_equal)
                eng.bn_aggr(mv[:, par, :], stats[:, par, :]).then_inc(s_mv, 1)
                eng.tensor_tensor(ohlo[:, par, :, :],
                                  iota[:, :].unsqueeze(1).to_broadcast([P, WPT, P]),
                                  lo[:, bass.ds(i * WPT, WPT)].unsqueeze(2).to_broadcast([P, WPT, P]),
                                  ALU.is_equal).then_inc(s_oh, 1)
                eng.wait_ge(s_sd, i + 1)
                eng.reciprocal(rstd[:, par:par + 1], sd[:, par:par + 1]).then_inc(s_rs, 1)
                eng.wait_ge(s_rs, i + 1)
                if not first:
                    eng.wait_ge(s_T, i - 1)
                eng.tensor_scalar(xh[:, par, :], xt[:, par, :], mv[:, par, 0:1], rstd[:, par:par + 1],
                                  ALU.subtract, ALU.mult).then_inc(s_xh, 1)
                eng.wait_ge(s_xh, i + 1)
                if not first:
                    eng.wait_ge(s_outR[par], 32 * j)
                eng.tensor_tensor(rowX[:, par, :], xt[:, par, :], xh[:, par, :], ALU.add).then_inc(s_base, 1)

            body(v, 0, 0)
            body(v, 0, 1)
            with v.Fori(1, NT // 2) as j:
                body(v, j, 0)
                body(v, j, 1)
            body(v, NT // 2, 0)

        @block.scalar
        def _(a):
            a.dma_start(att_in[:, :], row_bcast(att, D)).then_inc(s_att, 16)
            a.wait_ge(s_k, 1)

            def body(eng, j, par):
                i = 2 * j + par
                first = isinstance(j, int) and j == 0
                last = isinstance(j, int) and j > 0
                if first and par == 0:
                    eng.wait_ge(s_mv, 1)
                    eng.activation(sd[:, 0:1], mv[:, 0, 1:2], ACT.Sqrt, bias=k["eps"][:, 0:1]).then_inc(s_sd, 1)
                eng.wait_ge(s_T, i + 1)
                if not first:
                    eng.wait_ge(s_R, i - 1)
                eng.activation(xhT[:, par, :, :].rearrange("p k n -> p (k n)"), psT[:, par, :], ACT.Copy).then_inc(s_Tc, 1)
                if not last:
                    eng.wait_ge(s_mv, i + 2)
                    if not (first and par == 0):
                        eng.wait_ge(s_rs, i)
                    eng.activation(sd[:, 1 - par:2 - par], mv[:, 1 - par, 1:2], ACT.Sqrt,
                                   bias=k["eps"][:, 0:1]).then_inc(s_sd, 1)
                if not first:
                    eng.wait_ge(s_outL[par], 16 * j)
                    eng.wait_ge(s_outR[par], 32 * j)
                eng.wait_ge(s_L, i + 1)
                eng.activation(rowL[:, par, 0:D], psL[:, par, :], ACT.Copy).then_inc(s_Lc, 1)
                eng.wait_ge(s_R, i + 1)
                eng.activation(rowR[:, par, 0:D], psR[:, par, :], ACT.Copy).then_inc(s_Rc, 1)
                eng.activation(rowL[:, par, D:ROW], psA[:, par * 16:par * 16 + H], ACT.Copy)
                eng.activation(rowR[:, par, D:ROW], psA[:, par * 16 + H:par * 16 + 2 * H], ACT.Copy).then_inc(s_Ac, 1)

            body(a, 0, 0)
            body(a, 0, 1)
            with a.Fori(1, NT // 2) as j:
                body(a, j, 0)
                body(a, j, 1)
            body(a, NT // 2, 0)

        @block.tensor
        def _(t):
            t.wait_ge(s_k, 1)
            t.wait_ge(s_w, 32)

            def body(eng, j, par):
                i = 2 * j + par
                first = isinstance(j, int) and j == 0
                start = first and par == 0
                last = isinstance(j, int) and j > 0
                eng.wait_ge(s_xh, i + 1)
                if not first:
                    eng.wait_ge(s_Tc, i - 1)
                for c in range(KD):
                    ins = eng.transpose(psT[:, par, c * P:(c + 1) * P], xh[:, par, c * P:(c + 1) * P], k["ident"][:, :])
                ins.then_inc(s_T, 1)
                eng.wait_ge(s_oh, i + 1)
                for w in range(WPT):
                    ins = eng.matmul(psC[:, 0:NT], ohlo[:, par, w, :], ohhi[:, par, w, :],
                                     start=start and w == 0, stop=last and w == WPT - 1)
                ins.then_inc(s_cnt, 1)
                eng.wait_ge(s_Tc, i + 1)
                if start:
                    eng.wait_ge(s_wa, 1)
                if not first:
                    eng.wait_ge(s_Lc, i - 1)
                    eng.wait_ge(s_Rc, i - 1)
                    eng.wait_ge(s_Ac, i - 1)
                for c in range(KD):
                    ins = eng.matmul(psL[:, par, :], xhT[:, par, c, :], Wl[:, c, :], start=c == 0, stop=c == KD - 1)
                ins.then_inc(s_L, 1)
                for c in range(KD):
                    eng.matmul(psA[:, par * 16:par * 16 + 2 * H], xhT[:, par, c, :], Wa[:, c, :],
                               start=c == 0, stop=c == KD - 1)
                for c in range(KD):
                    ins = eng.matmul(psR[:, par, :], xhT[:, par, c, :], Wr[:, c, :], start=c == 0, stop=c == KD - 1)
                ins.then_inc(s_R, 1)

            body(t, 0, 0)
            body(t, 0, 1)
            with t.Fori(1, NT // 2) as j:
                body(t, j, 0)
                body(t, j, 1)
            body(t, NT // 2, 0)
    return m


def stage1b(nc, k, keep, dram):
    psC = keep["psC"]
    CH = BINS * NT // 7
    ctx = ExitStack()
    with ctx:
        m = Mem(nc, ctx, "sb")
        deg = m.sb("deg", [P, NT])
        tot = m.sb("tot", [P, NT])
        incl = m.sb("incl", [P, NT])
        first = m.sb("first_edge", [P, NT])
        key = m.sb("key", [P, NT])
        iob = m.sb("iota_bins", [P, BINS])
        M = m.sb("M", [P, BINS, NT], BF16)
        R = m.sb("R", [P, BINS, NT])
        T = m.sb("T", [P, BINS, NT])
        S = m.sb("S", [P, BINS, NT])
        pos = m.sb("pos", [P, NT])
        posi = m.sb("posi", [P, NT], I32)
        node = m.sb("node", [P, NT])
        nrec = m.sb("nrec", [P, NT, 4], I32)
        ordd = m.sb("ordd", [P, NT], I32)
        ordf = m.sb("ordf", [P, NT])
        K = m.sb("K", [P, NT])
        nsup = m.sb("nsup", [P, NT])
        cin = m.sb("cin", [P, NT])
        cex = m.sb("cex", [P, NT])
        nprev = m.sb("nprev", [P, NT])
        dK = m.sb("dK", [P, NT])
        iu = m.sb("iu", [P, UC])
        G1 = m.sb("G1", [P, UC, NT])
        G2 = m.sb("G2", [P, UC, NT])
        ut = m.sb("ut", [P, UC])
        ub = m.sb("ub", [P, UC])
        uk = m.sb("uk", [P, UC])
        un = m.sb("un", [P, UC])
        tmp = m.sb("tmp_u", [P, UC])
        urec = m.sb("urec", [P, UC, 4], I32)
        tu = m.sb("tu", [1, 2])
        tui = m.sb("tui", [1, 2], I32)
        psR = m.ps("psRank", (P, 2, 512))
        psT = m.ps("psTotal", (P, 2, 512))
        psN = m.ps("psNodes")

        ch_v = m.sem("sb_vector_chain")
        s_io = m.sem("sb_iotas")
        s_deg = m.sem("sb_degrees")
        s_pn = m.sem("sb_node_products")
        s_M = m.sem("sb_bin_masks")
        s_rank = m.sem("sb_ranks")
        s_rc = m.sem("sb_ranks_copied")
        s_nrec = m.sem("sb_node_records")
        s_scat = m.sem("sb_order_stored")
        s_ord = m.sem("sb_order_loaded")
        s_ordf = m.sem("sb_order_float")
        s_K = m.sem("sb_tile_maxima")
        s_u = m.sem("sb_unit_table")
        s_ust = m.sem("sb_unit_table_stored")

        block = ctx.enter_context(nc.Block())

        @block.gpsimd
        def _(g):
            g.iota(iob[:, :], pattern=[[1, BINS]], base=0, channel_multiplier=0,
                   allow_small_or_imprecise_dtypes=True).then_inc(s_io, 1)
            g.iota(node[:, :], pattern=[[P, NT]], base=0, channel_multiplier=1,
                   allow_small_or_imprecise_dtypes=True).then_inc(s_io, 1)
            g.iota(iu[:, :], pattern=[[P, UC]], base=0, channel_multiplier=1,
                   allow_small_or_imprecise_dtypes=True).then_inc(s_io, 1)
            g.wait_ge(s_nrec, 1)
            for c in range(NT):
                g.indirect_dma_start(dram["order"], bass.IndirectOffsetOnAxis(ap=posi[:, c:c + 1], axis=0),
                                     nrec[:, c, :], None).then_inc(s_scat, 16)
            g.wait_ge(s_ordf, 1)
            g.partition_all_reduce(K[:, :], ordf[:, :], P, bass.bass_isa.ReduceOp.max).then_inc(s_K, 1)

        @block.sync
        def _(sp):
            sp.wait_ge(s_scat, 16 * NT)
            with nc.allow_non_contiguous_dma(reason="one field of each node record"):
                sp.dma_start(ordd[:, :], dram["order"].rearrange("(t p) f -> p t f", p=P)[:, :, 2]).then_inc(s_ord, 16)
            sp.wait_ge(s_u, 1)
            sp.dma_start(dram["units"].rearrange("(c p) f -> p c f", p=P), urec[:, :, :]).then_inc(s_ust, 16)
            sp.wait_ge(s_ust, 16)

        @block.tensor
        def _(t):
            t.wait_ge(s_deg, 1)
            t.matmul(psN[:, 0:NT], k["upper"][:, :], deg[:, :], start=True, stop=True)
            t.matmul(psN[:, 64:64 + NT], k["ones"][:, :], deg[:, :], start=True, stop=True).then_inc(s_pn, 1)
            t.wait_ge(s_M, 1)
            Mf = M[:, :, :].rearrange("p b c -> p (b c)")
            for n in range(7):
                if n >= 2:
                    t.wait_ge(s_rc, n - 1)
                t.matmul(psR[:, n % 2, 0:CH], k["upper16"][:, :], Mf[:, n * CH:(n + 1) * CH], start=True, stop=True)
                t.matmul(psT[:, n % 2, 0:CH], k["ones16"][:, :], Mf[:, n * CH:(n + 1) * CH],
                         start=True, stop=True).then_inc(s_rank, 1)

        @block.scalar
        def _(a):
            Rf = R[:, :, :].rearrange("p b c -> p (b c)")
            Tf = T[:, :, :].rearrange("p b c -> p (b c)")
            for n in range(7):
                a.wait_ge(s_rank, n + 1)
                a.activation(Rf[:, n * CH:(n + 1) * CH], psR[:, n % 2, 0:CH], ACT.Copy)
                a.activation(Tf[:, n * CH:(n + 1) * CH], psT[:, n % 2, 0:CH], ACT.Copy).then_inc(s_rc, 1)

        @block.vector
        def _(v):
            ch = Chain(v, ch_v)
            v.tensor_copy(deg[:, :], psC[:, 0:NT]).then_inc(s_deg, 1)
            v.wait_ge(s_deg, 1)
            v.wait_ge(s_io, 3)
            ch(v.tensor_scalar(key[:, :], deg[:, :], float(BINS - 1), None, ALU.min))
            v.tensor_tensor(M[:, :, :], key[:, :].unsqueeze(1).to_broadcast([P, BINS, NT]),
                            iob[:, :].unsqueeze(2).to_broadcast([P, BINS, NT]), ALU.is_equal).then_inc(s_M, 1)
            v.wait_ge(s_pn, 1)
            ch(v.tensor_copy(tot[:, :], psN[:, 64:64 + NT]))
            ch(v.tensor_tensor_scan(incl[:, :], tot[:, :], tot[:, :], 0.0, ALU.add, ALU.bypass))
            ch(v.tensor_tensor(incl[:, :], incl[:, :], tot[:, :], ALU.subtract))
            ch(v.tensor_tensor(first[:, :], incl[:, :], psN[:, 0:NT], ALU.add))
            v.memset(nrec[:, :, 3], 0)
            v.tensor_copy(nrec[:, :, 0], node[:, :])
            v.tensor_copy(nrec[:, :, 1], first[:, :])
            ch(v.tensor_copy(nrec[:, :, 2], deg[:, :]))
            v.wait_ge(s_rc, 7)
            flat = lambda a: a[:, :, :].rearrange("p b c -> p (b c)")
            ch(v.tensor_tensor_scan(flat(S), flat(T), flat(T), 0.0, ALU.add, ALU.bypass))
            ch(v.tensor_tensor(flat(S), flat(S), flat(T), ALU.subtract))
            ch(v.tensor_tensor(flat(S), flat(S), flat(R), ALU.add))
            v.wait_ge(s_M, 1)
            ch(v.tensor_tensor(flat(S), flat(S), flat(M), ALU.mult))
            ch(v.tensor_reduce(pos[:, :], S[:, :, :].rearrange("p b c -> p c b"), AX.X, ALU.add))
            v.tensor_copy(posi[:, :], pos[:, :]).then_inc(s_nrec, 1)
            v.wait_ge(s_ord, 16)
            v.tensor_copy(ordf[:, :], ordd[:, :]).then_inc(s_ordf, 1)
            v.wait_ge(s_K, 1)
            ch(v.tensor_scalar(nsup[:, :], K[:, :], EDGES - 0.5, 1.0 / EDGES, ALU.add, ALU.mult))
            ch(v.tensor_scalar(nsup[:, :], nsup[:, :], -0.5, ROUND, ALU.add, ALU.add))
            ch(v.tensor_scalar(nsup[:, :], nsup[:, :], -ROUND, 1.0, ALU.add, ALU.max))
            ch(v.tensor_tensor_scan(cin[:, :], nsup[:, :], nsup[:, :], 0.0, ALU.add, ALU.bypass))
            v.tensor_tensor(cex[:, :], cin[:, :], nsup[:, :], ALU.subtract)
            v.memset(nprev[:, 0:1], 0.0)
            v.tensor_copy(nprev[:, 1:NT], nsup[:, 0:NT - 1])
            v.tensor_copy(dK[:, 0:1], K[:, 0:1])
            ch(v.tensor_tensor(dK[:, 1:NT], K[:, 1:NT], K[:, 0:NT - 1], ALU.subtract))
            u3 = lambda a: a[:, :].unsqueeze(1).to_broadcast([P, UC, NT])
            ch(v.tensor_tensor(G1[:, :, :], iu[:, :].unsqueeze(2).to_broadcast([P, UC, NT]), u3(cex), ALU.is_ge))
            ch(v.tensor_reduce(ut[:, :], G1[:, :, :], AX.X, ALU.add))
            ch(v.tensor_tensor(G2[:, :, :], G1[:, :, :], u3(nprev), ALU.mult))
            ch(v.tensor_reduce(ub[:, :], G2[:, :, :], AX.X, ALU.add))
            ch(v.tensor_tensor(G2[:, :, :], G1[:, :, :], u3(dK), ALU.mult))
            ch(v.tensor_reduce(uk[:, :], G2[:, :, :], AX.X, ALU.add))
            ch(v.tensor_tensor(ub[:, :], iu[:, :], ub[:, :], ALU.subtract))
            ch(v.tensor_scalar(ub[:, :], ub[:, :], float(EDGES), None, ALU.mult))
            ch(v.tensor_tensor(uk[:, :], uk[:, :], ub[:, :], ALU.subtract))
            ch(v.memset(un[:, :], float(GB[1])))
            for g in range(1, NG):
                ch(v.tensor_scalar(tmp[:, :], uk[:, :], float(GB[g]), float(GB[g + 1] - GB[g]), ALU.is_ge, ALU.mult))
                ch(v.tensor_tensor(un[:, :], un[:, :], tmp[:, :], ALU.add))
            ch(v.tensor_scalar(ut[:, :], ut[:, :], -1.0, float(P), ALU.add, ALU.mult))
            v.tensor_copy(urec[:, :, 0], ut[:, :])
            v.tensor_copy(urec[:, :, 1], un[:, :])
            v.tensor_copy(urec[:, :, 2], ub[:, :])
            v.tensor_scalar(urec[:, :, 3], un[:, :], -float(FIX), None, ALU.add).then_inc(s_u, 1)
            ch(v.tensor_scalar(tu[0:1, 0:1], cin[0:1, NT - 1:NT], 1.0 - 2 * PEELED, None, ALU.add))
            ch(v.tensor_copy(tui[0:1, 0:1], tu[0:1, 0:1]))
            ch(v.tensor_scalar(keep["rounds"][0:1, 0:1], tui[0:1, 0:1], 1, None, ALU.arith_shift_right))
    return m


def stage2(nc, k, keep, dram, ins):
    src, bias = ins["src"], ins["bias"]
    SRC_LEN = src.shape[1]
    ctx = ExitStack()
    with ctx:
        m = Mem(nc, ctx, "s2")
        G = [m.sb(f"G{i}", [P, SLOTS, ROW]) for i in range(2)]
        Z = m.sb("Z", [P, SLOTS + 1, D])
        T = m.sb("T", [P, 2, WMAX, D])
        zT = m.sb("zT", [P, 3, KD, P])
        attT = m.sb("attT", [P, KD])
        attB = m.sb("attB", [P, KD, 2])
        xrow = m.sb("xrow", [P, 2, ROW])
        nb = m.sb("nb", [P, 2, D])
        urec = m.sb("urec", [P, 2, 4], I32)
        nrec = m.sb("nrec", [P, 2, 4], I32)
        srec = m.sb("srec", [1, 2, 4], I32)
        nid = m.sb("nid", [P, 2], I32)
        start = m.sb("start", [P, 2], I32)
        runs = m.sb("runs", [P, 2, EDGES], I32)
        raw = m.sb("raw", [P, SLOTS, H])
        score = m.sb("score", [P, SLOTS, H])
        expin = m.sb("expin", [P, SLOTS + 1, H])
        ea = m.sb("ea", [P, SLOTS + 1, H])
        slot = m.sb("slot", [P, SLOTS])
        left = m.sb("left", [P, 1])
        off = m.sb("off", [P, SLOTS])
        fresh = m.sb("fresh", [P, 1])
        peak = m.sb("peak", [P, H])
        mx = m.sb("mx", [P, H])
        mold = m.sb("mold", [P, H])
        csum = m.sb("csum", [P, H])
        den = m.sb("den", [P, H])
        rden = m.sb("rden", [P, H])
        acc = m.sb("acc", [P, D])
        o = m.sb("o", [P, D])
        orelu = m.sb("orelu", [P, D])
        oexp = m.sb("oexp", [P, D])
        xn = m.sb("xn", [P, 2, D])
        biasb = m.sb("biasb", [P, D])
        nil = m.sb("nil", [P, 4 * NG])
        psA = m.ps("psAcc", (P, 2, 512))
        psZ = m.ps("psZ", (P, 3, 512))
        psS = m.ps("psScore", (P, 2, 512))
        psN = m.ps("psNil")

        s_bias = m.sem("s2_bias_loaded")
        s_init = m.sem("s2_initialised")
        s_attB = m.sem("s2_att_chunks")
        s_gate = m.sem("s2_gate")
        s_slot = m.sem("s2_slot_numbers")
        s_urec = [m.sem(f"s2_unit_record_loaded{i}") for i in range(2)]
        s_nrec = [m.sem(f"s2_node_record_loaded{i}") for i in range(2)]
        s_srec = [m.sem(f"s2_store_record_loaded{i}") for i in range(2)]
        s_read = m.sem("s2_unit_record_read_by_tensor")
        s_start = m.sem("s2_run_starts")
        s_runs = [m.sem(f"s2_runs_loaded{i}") for i in range(2)]
        s_rowL = [m.sem(f"s2_left_rows_added{i}") for i in range(2)]
        s_rowF = [m.sem(f"s2_first_left_rows_added{i}") for i in range(2)]
        s_rowR = [m.sem(f"s2_right_rows_loaded{i}") for i in range(2)]
        s_rowX = [m.sem(f"s2_residual_rows_loaded{i}") for i in range(2)]
        s_fill = [m.sem(f"s2_filled_group{g}") for g in range(NG)]
        s_nb = m.sem("s2_bias_less_right_rows")
        s_zT = m.sem("s2_slot_transposed")
        s_rz = m.sem("s2_transposed_relu")
        s_sc = m.sem("s2_transposed_scored")
        s_mask = m.sem("s2_masks")
        s_att = [m.sem(f"s2_times_att_group{g}") for g in range(NG)]
        s_scored = m.sem("s2_first_scores_taken")
        s_wt = [m.sem(f"s2_weighted_group{g}") for g in range(NG)]
        s_wacc = m.sem("s2_carried_sum_weighted")
        s_add = [m.sem(f"s2_added_group{g}") for g in range(NG)]
        s_closed = m.sem("s2_sums_closed")
        s_acc = m.sem("s2_sum_carried")
        s_st = [m.sem(f"s2_statistics_step{n}") for n in range(8)]
        s_expin = m.sem("s2_exponents")
        s_ea = m.sem("s2_exponentials")
        s_den = [m.sem(f"s2_denominator_step{n}") for n in range(4)]
        s_ep = [m.sem(f"s2_result_step{n}") for n in range(2)]
        s_o = m.sem("s2_output_rows")
        s_oe = m.sem("s2_output_exponentials")
        s_xn = m.sem("s2_new_rows")
        s_xnst = [m.sem(f"s2_new_rows_stored{i}") for i in range(2)]

        def firm(eng):
            eng.sem_inc(s_gate, 1)

        def units(eng, body):
            more = eng.value_load(keep["rounds"][0:1, 0:1], min_val=NT // 2 - PEELED, max_val=UC * P // 2 - PEELED)
            for i in range(2 * PEELED - 1):
                body(i, i // 2, i % 2, False)
            with eng.Fori(PEELED, more + PEELED) as j:
                body(2 * j - 1, j - 1, 1, False)
                body(2 * j, j, 0, False)
            body(2 * more + 2 * PEELED - 1, more + PEELED - 1, 1, True)
            return 2 * more + 2 * PEELED - 1, more + PEELED - 1

        def slots_of(eng, par):
            firm(eng)
            return eng.value_load(urec[0:1, par, 1:2], min_val=GB[1], max_val=SLOTS)

        def group(a, g):
            return a[:, GB[g]:GB[g + 1], :]

        block = ctx.enter_context(nc.Block())

        @block.sync
        def _(sp):
            sp.dma_start(biasb[:, :], row_bcast(bias, D)).then_inc(s_bias, 16)
            sp.dma_start(attT[:, :], ins["att"].rearrange("(k p) -> p k", p=P), allow_slow_non_contiguous=True).then_inc(s_bias, 16)

            def store(i, q, par):
                sp.dma_start(srec[:, par, :], dram["units"][bass.ds(i, 1), :]).then_inc(s_srec[par], 16)
                sp.wait_ge(s_srec[par], 16 * (q + 1))
                firm(sp)
                row = sp.value_load(srec[0:1, par, 0:1], min_val=0, max_val=NP - P)
                sp.wait_ge(s_xn, i + 1)
                after(sp, s_xnst[1 - par], 16 * (q + par))
                sp.dma_start(dram["xnew"][bass.ds(row, P), :], xn[:, par, :]).then_inc(s_xnst[par], 16)

            def body(i, q, par, last):
                after(sp, s_mask, i - 1)
                after(sp, s_read, i - 1)
                after(sp, s_start, i - 1)
                sp.dma_start(urec[:, par, :], dram["units"][bass.ds(i, 1), :].to_broadcast([P, 4])).then_inc(s_urec[par], 16)
                sp.wait_ge(s_urec[par], 16 * (q + 1))
                firm(sp)
                row = sp.value_load(urec[0:1, par, 0:1], min_val=0, max_val=NP - P)
                sp.dma_start(nrec[:, par, :], dram["order"][bass.ds(row, P), :]).then_inc(s_nrec[par], 16)
                if not (isinstance(i, int) and i < 3):
                    store(i - 3, q - 2 + par, 1 - par)
            i, q = units(sp, body)
            store(i - 2, q - 1, 1)
            store(i - 1, q, 0)
            store(i, q, 1)
            sp.wait_ge(s_xnst[0], 16 * (q + 1))
            sp.wait_ge(s_xnst[1], 16 * (q + 1))
            firm(sp)

        @block.gpsimd
        def _(g_):
            g_.iota(slot[:, :], pattern=[[1, SLOTS]], base=-1, channel_multiplier=0,
                    allow_small_or_imprecise_dtypes=True).then_inc(s_slot, 1)
            g_.wait_ge(s_bias, 32)

            def residual(i, q, par):
                after(g_, s_xnst[par], 16 * q)
                firm(g_)
                g_.indirect_dma_start(xn[:, par, :], None, dram["rowX"],
                                      bass.IndirectOffsetOnAxis(ap=nid[:, par:par + 1], axis=0)).then_inc(s_rowX[par], 16)

            def body(i, q, par, last):
                g_.wait_ge(s_urec[par], 16 * (q + 1))
                g_.wait_ge(s_nrec[par], 16 * (q + 1))
                ns = slots_of(g_, par)
                after(g_, s_rowX[par], 16 * q)
                firm(g_)
                g_.tensor_copy(nid[:, par:par + 1], nrec[:, par, 0:1])
                g_.tensor_scalar(start[:, par:par + 1], nrec[:, par, 1:2], urec[:, par, 2:3], float(SRC_LEN - EDGES),
                                 ALU.add, ALU.min).then_inc(s_start, 1)
                g_.wait_ge(s_start, i + 1)
                after(g_, s_fill[NG - 1], i - 1)
                after(g_, s_nb, i - 1)
                firm(g_)
                g_.indirect_dma_start(runs[:, par, :], None, src,
                                      bass.IndirectOffsetOnAxis(ap=start[:, par:par + 1], axis=1)).then_inc(s_runs[par], 16)
                g_.indirect_dma_start(xrow[:, par, :], None, dram["rowR"],
                                      bass.IndirectOffsetOnAxis(ap=nid[:, par:par + 1], axis=0)).then_inc(s_rowR[par], 16)
                g_.wait_ge(s_runs[par], 16 * (q + 1))
                firm(g_)

                def gather(g, sem):
                    g_.wait_ge(s_fill[g], i + 1)
                    firm(g_)
                    for s in range(GB[g], GB[g + 1]):
                        ids = runs[:, par, s - 1:s] if s else nid[:, par:par + 1]
                        g_.indirect_dma_start(G[par][:, s, :], None, dram["rowL"], bass.IndirectOffsetOnAxis(ap=ids, axis=0),
                                              compute_op=ALU.add).then_inc(sem, 16)
                gather(0, s_rowF[par])
                if not (isinstance(i, int) and i == 0):
                    residual(i - 1, q - 1 + par, 1 - par)
                for g in range(1, NG):
                    with g_.If(ns > GB[g]):
                        gather(g, s_rowL[par])
                g_.wait_ge(s_rowR[par], 16 * (q + 1))
                after(g_, s_o, i - 1)
                g_.tensor_tensor(nb[:, par, :], biasb[:, :], xrow[:, par, 0:D], ALU.subtract).then_inc(s_nb, 1)
            i, q = units(g_, body)
            residual(i, q, 1)

        @block.scalar
        def _(a):
            a.wait_ge(s_init, 1)

            def fill(i, q, par):
                a.wait_ge(s_rowR[par], 16 * (q + 1))
                for g in range(NG):
                    w = GB[g + 1] - GB[g]
                    after(a, s_wt[g], i - 1)
                    if g == 0:
                        after(a, s_zT, FIX * (i - 1))
                    a.activation(group(G[par], g), xrow[:, par, :].unsqueeze(1).to_broadcast([P, w, ROW]),
                                 ACT.Copy).then_inc(s_fill[g], 1)

            def relu(i):
                for s in range(FIX):
                    a.wait_ge(s_zT, FIX * i + s + 1)
                    after(a, s_sc, FIX * i + s - 2)
                    a.activation(zT[:, s % 3, :, :].rearrange("p k n -> p (k n)"), psZ[:, s % 3, :], ACT.Relu).then_inc(s_rz, 1)

            def body(i, q, par, last):
                begin = isinstance(i, int) and i == 0
                if not last:
                    fill(i + 1, q + par, 1 - par)
                if not begin:
                    carry(i - 1, 1 - par)
                a.wait_ge(s_expin, i + 1)
                a.activation(ea[:, :, :], expin[:, :, :], ACT.Exp).then_inc(s_ea, 1)
                if not begin:
                    result(i - 1)
                if not last:
                    relu(i + 1)

            def carry(i, par):
                a.wait_ge(s_closed, i + 1)
                a.wait_ge(s_wacc, i + 1)
                a.activation(acc[:, :], psA[:, par, :], ACT.Copy).then_inc(s_acc, 1)

            def result(i):
                a.wait_ge(s_o, i + 1)
                a.activation(orelu[:, :], o[:, :], ACT.Relu)
                a.activation(oexp[:, :], o[:, :], ACT.Exp).then_inc(s_oe, 1)
            fill(0, 0, 0)
            relu(0)
            i, q = units(a, body)
            carry(i, 1)
            result(i)

        @block.tensor
        def _(t):
            t.wait_ge(s_attB, 1)

            def scores(i, q, par):
                t.wait_ge(s_rowF[par], 16 * FIX * (q + 1))

                def product(s):
                    t.wait_ge(s_rz, FIX * i + s + 1)
                    if s == 0:
                        after(t, s_scored, i - 1)
                    for c in range(KD):
                        ins_ = t.matmul(psS[:, par, s * H + 2 * c:s * H + 2 * c + 2], zT[:, s % 3, c, :], attB[:, c, :],
                                        start=True, stop=True)
                    ins_.then_inc(s_sc, 1)
                for s in range(FIX):
                    after(t, s_rz, FIX * i + s - 2)
                    for c in range(KD):
                        ins_ = t.transpose(psZ[:, s % 3, c * P:(c + 1) * P], G[par][:, s, c * P:(c + 1) * P], k["ident"][:, :])
                    ins_.then_inc(s_zT, 1)
                    if s >= 2:
                        product(s - 2)
                product(FIX - 2)
                product(FIX - 1)

            def body(i, q, par, last):
                t.wait_ge(s_urec[par], 16 * (q + 1))
                ns = slots_of(t, par)
                t.sem_inc(s_read, 1)
                if not last:
                    scores(i + 1, q + par, 1 - par)
                after(t, s_acc, i - 1)
                for g in range(NG):
                    def add():
                        t.wait_ge(s_wt[g], i + 1)
                        for s in range(GB[g], GB[g + 1]):
                            ins = t.matmul(psA[:, par, :], k["ident"][:, :], Z[:, s, :], start=s == 0, stop=False)
                        ins.then_inc(s_add[g], 1)
                    if g == 0:
                        add()
                        continue
                    with t.If(ns > GB[g]):
                        add()
                    with t.Else():
                        t.matmul(psN[:, par * NG + g:par * NG + g + 1], k["ones16"][:, :], k["ones16"][:, 0:1], start=True, stop=True).then_inc(s_add[g], 1)
                t.wait_ge(s_wacc, i + 1)
                t.matmul(psA[:, par, :], k["ident"][:, :], Z[:, SLOTS, :], start=False, stop=True).then_inc(s_closed, 1)
            scores(0, 0, 0)
            units(t, body)

        @block.vector
        def _(v):
            v.memset(nil[:, :], 0.0)
            v.memset(attB[:, :, :], 0.0)
            v.memset(raw[:, :, :], 0.0)
            v.memset(mx[:, :], 0.0)
            v.memset(den[:, :], 0.0)
            v.memset(acc[:, :], 0.0)
            v.memset(rden[:, :], 0.0).then_inc(s_init, 1)
            v.wait_ge(s_init, 1)
            v.wait_ge(s_slot, 1)
            v.wait_ge(s_bias, 32)
            for n in range(2):
                rows = slice(n * C, (n + 1) * C)
                ins_ = v.tensor_scalar(attB[rows, :, n], attT[rows, :], 1.0 - SLOPE, None, ALU.mult)
            ins_.then_inc(s_attB, 1)
            arrived = [v.alloc_register(f"rows_arrived{p}") for p in range(2)]
            for r in arrived:
                v.reg_mov(r, 0)
            heads = lambda ap: ap.rearrange("p (h c) -> p h c", c=C)
            over = lambda ap: ap.unsqueeze(2).to_broadcast([P, H, C])

            def result1(i, par):
                v.wait_ge(s_acc, i + 1)
                v.tensor_tensor(heads(o[:, :]), heads(acc[:, :]), over(rden[:, :]), ALU.mult).then_inc(s_ep[0], 1)
                v.wait_ge(s_ep[0], i + 1)
                v.wait_ge(s_nb, i + 1)
                v.tensor_tensor(o[:, :], o[:, :], nb[:, par, :], ALU.add).then_inc(s_o, 1)

            def result2(i, q, par):
                v.wait_ge(s_oe, i + 1)
                v.scalar_tensor_tensor(o[:, :], oexp[:, :], 1.0, orelu[:, :], ALU.min, ALU.add).then_inc(s_ep[1], 1)
                v.wait_ge(s_ep[1], i + 1)
                v.wait_ge(s_rowX[par], 16 * (q + 1))
                v.scalar_tensor_tensor(xn[:, par, :], o[:, :], -1.0, xn[:, par, :], ALU.add, ALU.add).then_inc(s_xn, 1)

            def body(i, q, par, last):
                n = i + 1
                begin = isinstance(i, int) and i == 0
                v.wait_ge(s_urec[par], 16 * (q + 1))
                v.wait_ge(s_nrec[par], 16 * (q + 1))
                ns = slots_of(v, par)
                beyond = v.value_load(urec[0:1, par, 3:4], min_val=0, max_val=SLOTS - FIX)
                st = iter(s_st)

                def step(ins):
                    s = next(st)
                    ins.then_inc(s, 1)
                    v.wait_ge(s, n)

                def when(g, do, sem, kind):
                    at = (2 * kind + par) * NG + g
                    if g == 0:
                        do()
                        return
                    with v.If(ns > GB[g]):
                        do()
                    with v.Else():
                        v.memset(nil[0:1, at:at + 1], 0.0).then_inc(sem, 1)

                v.tensor_tensor(left[:, :], nrec[:, par, 2:3], urec[:, par, 2:3], ALU.subtract)
                step(v.tensor_scalar(fresh[:, :], urec[:, par, 2:3], 0.0, -NEG, ALU.is_equal, ALU.mult))
                v.tensor_scalar(mold[:, :], mx[:, :], fresh[:, 0:1], None, ALU.add)
                step(v.tensor_scalar(off[:, :], slot[:, :], left[:, 0:1], 1.0, ALU.is_lt, ALU.subtract))
                v.tensor_scalar(off[:, 0:1], urec[:, par, 2:3], 0.0, -1.0, ALU.is_gt, ALU.mult).then_inc(s_mask, 1)
                v.wait_ge(s_mask, n)
                firm(v)
                for g in range(1, NG):
                    def times_att():
                        w = GB[g + 1] - GB[g]
                        if g == 1:
                            v.reg_add(arrived[par], arrived[par], v.to_reg(beyond * 16))
                            v.wait_ge(s_rowL[par], v.snap(arrived[par]))
                        v.scalar_tensor_tensor(T[:, g % 2, 0:w, :], group(G[par], g)[:, :, 0:D], 0.0,
                                               keep["att"][:, :].unsqueeze(1).to_broadcast([P, w, D]), ALU.max, ALU.mult
                                               ).then_inc(s_att[g], 1)
                        v.wait_ge(s_att[g], n)
                        v.tensor_reduce(group(raw, g), T[:, g % 2, 0:w, :].rearrange("p s (h c) -> p s h c", c=C), AX.X, ALU.add)
                    when(g, times_att, s_att[g], 0)
                v.wait_ge(s_fill[NG - 1], n)
                v.wait_ge(s_rowF[par], 16 * FIX * (q + 1))
                v.wait_ge(s_sc, FIX * n)
                v.tensor_tensor(score[:, 0:FIX, :], psS[:, par, 0:FIX * H].rearrange("p (s h) -> p s h", h=H),
                                G[par][:, 0:FIX, D:ROW], ALU.add).then_inc(s_scored, 1)
                v.wait_ge(s_scored, n)
                step(v.tensor_tensor(score[:, FIX:SLOTS, :], raw[:, FIX:SLOTS, :], G[par][:, FIX:SLOTS, D:ROW], ALU.add))
                step(v.scalar_tensor_tensor(score[:, :, :], off[:, :].unsqueeze(2).to_broadcast([P, SLOTS, H]), NEG,
                                            score[:, :, :], ALU.mult, ALU.add))
                step(v.tensor_reduce(peak[:, :], score[:, :, :].rearrange("p s h -> p h s"), AX.X, ALU.max))
                step(v.tensor_tensor(mx[:, :], mold[:, :], peak[:, :], ALU.max))
                v.tensor_tensor(expin[:, SLOTS, :], mold[:, :], mx[:, :], ALU.subtract)
                v.tensor_tensor(expin[:, 0:SLOTS, :], score[:, :, :],
                                mx[:, :].unsqueeze(1).to_broadcast([P, SLOTS, H]), ALU.subtract).then_inc(s_expin, 1)
                if not begin:
                    result1(i - 1, 1 - par)
                v.wait_ge(s_ea, n)
                for g in range(NG):
                    def weigh():
                        w = GB[g + 1] - GB[g]
                        after(v, s_add[g], i)
                        v.tensor_tensor(group(Z, g).rearrange("p s (h c) -> p s h c", c=C),
                                        group(G[par], g)[:, :, 0:D].rearrange("p s (h c) -> p s h c", c=C),
                                        group(ea, g).unsqueeze(3).to_broadcast([P, w, H, C]), ALU.mult).then_inc(s_wt[g], 1)
                    when(g, weigh, s_wt[g], 1)
                after(v, s_acc, i)
                v.tensor_tensor(heads(Z[:, SLOTS, :]), heads(acc[:, :]), over(ea[:, SLOTS, :]), ALU.mult).then_inc(s_wacc, 1)
                v.tensor_reduce(csum[:, :], ea[:, 0:SLOTS, :].rearrange("p s h -> p h s"), AX.X, ALU.add)
                v.tensor_tensor(den[:, :], den[:, :], ea[:, SLOTS, :], ALU.mult).then_inc(s_den[0], 1)
                v.wait_ge(s_den[0], n)
                v.tensor_tensor(den[:, :], den[:, :], csum[:, :], ALU.add).then_inc(s_den[1], 1)
                v.wait_ge(s_den[1], n)
                v.tensor_scalar(rden[:, :], den[:, :], 1e-16, None, ALU.max).then_inc(s_den[2], 1)
                v.wait_ge(s_den[2], n)
                v.reciprocal(rden[:, :], rden[:, :]).then_inc(s_den[3], 1)
                v.wait_ge(s_den[3], n)
                if not begin:
                    result2(i - 1, q - 1 + par, 1 - par)
            i, q = units(v, body)
            v.wait_ge(s_xn, i)
            result1(i, 1)
            result2(i, q, 1)
    return m


def node_tiles(eng, body):
    body(eng, 0, 0)
    body(eng, 0, 1)
    with eng.Fori(1, NT // 2) as j:
        body(eng, j, 0)
        body(eng, j, 1)
    body(eng, NT // 2, 0)


def stage3(nc, k, keep, dram, ins):
    Wg, bg = ins["Wg"], ins["bg"]
    NX = NT * X
    ctx = ExitStack()
    with ctx:
        m = Mem(nc, ctx, "s3")
        Wgs = m.sb("Wg", [P, KD, X])
        bgb = m.sb("bg", [P, X])
        xt = m.sb("xt", [P, 2, D])
        xh = m.sb("xh", [P, 2, D])
        xhT = m.sb("xhT", [P, 2, KD, P])
        stats = m.sb("stats", [P, 2, 6])
        mv = m.sb("mv", [P, 2, 2])
        sd = m.sb("sd", [P, 2])
        rstd = m.sb("rstd", [P, 2])
        lg = m.sb("logits", [P, NT, X])
        pr = m.sb("probs", [P, NT, X])
        M = [m.sb(f"chosen{n}", [P, NT, X]) for n in range(2)]
        tmp = m.sb("tmp", [P, NT, X])
        io = m.sb("iota_x", [P, X])
        back = m.sb("iota_back", [P, X])
        top = m.sb("top", [P, NT])
        both = m.sb("both", [P, X, NT], BF16)
        S = m.sb("S", [P, X, NT])
        R = m.sb("R", [P, X, NT])
        T = m.sb("T", [P, X, NT])
        begin = m.sb("begin", [P, X + 1])
        nt = m.sb("nt", [P, X])
        ntc = m.sb("ntc", [P, X])
        base = m.sb("base", [P, X])
        posf = m.sb("posf", [P, NT])
        rowid = m.sb("rowid", [P, NT], I32)
        tj = m.sb("tj", [P, TILES])
        tc = m.sb("tc", [P, TILES, X])
        te = m.sb("te", [P, TILES])
        zi = m.sb("zi", [P, TILES], I32)
        psT = m.ps("psT", (P, 2, 512))
        psG = m.ps("psG")
        psR = m.ps("psRank", (P, 2, 512))
        psS = m.ps("psTotal", (P, 2, 512))

        s_w = m.sem("s3_router_loaded")
        s_x = [m.sem(f"s3_x_loaded{i}") for i in range(2)]
        s_bn = m.sem("s3_stats")
        s_mv = m.sem("s3_mean_var")
        s_sd = m.sem("s3_std")
        s_rs = m.sem("s3_rstd")
        s_xh = m.sem("s3_normed")
        s_T = m.sem("s3_transposed")
        s_Tc = m.sem("s3_transposed_copied")
        s_G = m.sem("s3_router_product")
        s_lg = m.sem("s3_logits")
        s_h = [m.sem(f"s3_normed_stored{i}") for i in range(2)]
        s_io = m.sem("s3_iotas")
        ch_v = m.sem("s3_vector_chain")
        s_ein = m.sem("s3_exponents")
        s_ex = m.sem("s3_exponentials")
        s_both = m.sem("s3_choices")
        s_rank = m.sem("s3_ranks")
        s_rc = m.sem("s3_ranks_copied")
        s_zi = m.sem("s3_zero_ids")
        s_zst = m.sem("s3_row_ids_cleared")
        s_pos = m.sem("s3_places")
        s_scat = m.sem("s3_row_ids_stored")

        xv = dram["xnew"].rearrange("(t p) d -> t p d", p=P)
        hv = dram["hrow"].rearrange("(t p) d -> t p d", p=P)
        block = ctx.enter_context(nc.Block())

        @block.sync
        def _(sp):
            sp.dma_start(Wgs[:, :, :], Wg.rearrange("(k p) n -> p k n", p=P)).then_inc(s_w, 16)
            sp.dma_start(bgb[:, :], row_bcast(bg, X)).then_inc(s_w, 16)

            def body(eng, j, par):
                i = 2 * j + par
                if not (isinstance(j, int) and j == 0):
                    eng.wait_ge(s_xh, i - 1)
                eng.dma_start(xt[:, par, :], xv[i, :, :]).then_inc(s_x[par], 16)
            node_tiles(sp, body)
            sp.dma_start(keep["W1"][:, :, :], ins["W1"].rearrange("e (k p) n -> p (e k) n", p=P)).then_inc(keep["s_W"], 16)
            sp.dma_start(keep["W2"][:, :, :], ins["W2"].rearrange("e (k p) n -> p (e k) n", p=P)).then_inc(keep["s_W"], 16)

        @block.gpsimd
        def _(g):
            g.iota(io[:, :], pattern=[[1, X]], base=0, channel_multiplier=0, allow_small_or_imprecise_dtypes=True).then_inc(s_io, 1)
            g.iota(back[:, :], pattern=[[-1, X]], base=X, channel_multiplier=0, allow_small_or_imprecise_dtypes=True).then_inc(s_io, 1)
            g.iota(rowid[:, :], pattern=[[P, NT]], base=0, channel_multiplier=1).then_inc(s_io, 1)
            g.iota(tj[:, :], pattern=[[1, TILES]], base=0, channel_multiplier=0, allow_small_or_imprecise_dtypes=True).then_inc(s_io, 1)
            g.memset(zi[:, :], 0).then_inc(s_zi, 1)
            g.wait_ge(s_zi, 1)
            g.dma_start(dram["slots"].rearrange("(p j) a -> p (j a)", p=P), zi[:, :]).then_inc(s_zst, 16)
            g.wait_ge(s_zst, 16)
            g.wait_ge(s_io, 3)
            for n in range(2):
                g.wait_ge(s_pos, n + 1)
                for c in range(NT):
                    g.indirect_dma_start(dram["slots"], bass.IndirectOffsetOnAxis(ap=keep["pos"][n][:, c:c + 1], axis=0),
                                         rowid[:, c:c + 1], None).then_inc(s_scat, 16)
            g.wait_ge(s_scat, 16 * 2 * NT)

        @block.tensor
        def _(t):
            t.wait_ge(s_w, 32)

            def body(eng, j, par):
                i = 2 * j + par
                first = isinstance(j, int) and j == 0
                eng.wait_ge(s_xh, i + 1)
                if not first:
                    eng.wait_ge(s_Tc, i - 1)
                for c in range(KD):
                    ins_ = eng.transpose(psT[:, par, c * P:(c + 1) * P], xh[:, par, c * P:(c + 1) * P], k["ident"][:, :])
                ins_.then_inc(s_T, 1)
                eng.wait_ge(s_Tc, i + 1)
                if not first:
                    eng.wait_ge(s_lg, i - 1)
                for c in range(KD):
                    ins_ = eng.matmul(psG[:, par * X:(par + 1) * X], xhT[:, par, c, :], Wgs[:, c, :], start=c == 0, stop=c == KD - 1)
                ins_.then_inc(s_G, 1)
            node_tiles(t, body)
            t.wait_ge(s_both, 1)
            bf = both[:, :, :].rearrange("p e c -> p (e c)")
            for n in range(2):
                w = slice(n * NX // 2, (n + 1) * NX // 2)
                t.matmul(psR[:, n, 0:NX // 2], k["upper16"][:, :], bf[:, w], start=True, stop=True)
                t.matmul(psS[:, n, 0:NX // 2], k["ones16"][:, :], bf[:, w], start=True, stop=True).then_inc(s_rank, 1)

        @block.scalar
        def _(a):
            def body(eng, j, par):
                i = 2 * j + par
                first = isinstance(j, int) and j == 0
                last = isinstance(j, int) and j > 0
                if first and par == 0:
                    eng.wait_ge(s_mv, 1)
                    eng.activation(sd[:, 0:1], mv[:, 0, 1:2], ACT.Sqrt, bias=k["eps"][:, 0:1]).then_inc(s_sd, 1)
                eng.wait_ge(s_T, i + 1)
                if not first:
                    eng.wait_ge(s_G, i - 1)
                eng.activation(xhT[:, par, :, :].rearrange("p k n -> p (k n)"), psT[:, par, :], ACT.Copy).then_inc(s_Tc, 1)
                if not last:
                    eng.wait_ge(s_mv, i + 2)
                    if not (first and par == 0):
                        eng.wait_ge(s_rs, i)
                    eng.activation(sd[:, 1 - par:2 - par], mv[:, 1 - par, 1:2], ACT.Sqrt,
                                   bias=k["eps"][:, 0:1]).then_inc(s_sd, 1)
                eng.wait_ge(s_xh, i + 1)
                eng.dma_start(hv[i, :, :], xh[:, par, :]).then_inc(s_h[par], 16)
            node_tiles(a, body)
            a.wait_ge(s_ein, 1)
            a.activation(pr[:, :, :], lg[:, :, :], ACT.Exp).then_inc(s_ex, 1)
            Rf, Tf = (z[:, :, :].rearrange("p e c -> p (e c)") for z in (R, T))
            for n in range(2):
                w = slice(n * NX // 2, (n + 1) * NX // 2)
                a.wait_ge(s_rank, n + 1)
                a.activation(Rf[:, w], psR[:, n, 0:NX // 2], ACT.Copy)
                a.activation(Tf[:, w], psS[:, n, 0:NX // 2], ACT.Copy).then_inc(s_rc, 1)
            for par in range(2):
                a.wait_ge(s_h[par], 16 * ((NT + 1 - par) // 2))

        @block.vector
        def _(v):
            v.wait_ge(s_w, 32)

            def body(eng, j, par):
                i = 2 * j + par
                first = isinstance(j, int) and j == 0
                eng.wait_ge(s_x[par], 16 * (j + 1))
                eng.bn_stats(stats[:, par, :], xt[:, par, :]).then_inc(s_bn, 1)
                if not (first and par == 0):
                    eng.wait_ge(s_G, i)
                    eng.tensor_tensor(lg[:, bass.ds(i - 1, 1), :], psG[:, (1 - par) * X:(2 - par) * X].unsqueeze(1),
                                      bgb[:, :].unsqueeze(1), ALU.add).then_inc(s_lg, 1)
                    eng.wait_ge(s_bn, i + 1)
                    eng.tensor_copy(mvnil[:, :], stats[:, par, 0:1])
                else:
                    eng.wait_ge(s_bn, 1)
                eng.bn_aggr(mv[:, par, :], stats[:, par, :]).then_inc(s_mv, 1)
                eng.wait_ge(s_sd, i + 1)
                eng.reciprocal(rstd[:, par:par + 1], sd[:, par:par + 1]).then_inc(s_rs, 1)
                eng.wait_ge(s_rs, i + 1)
                if not first:
                    eng.wait_ge(s_T, i - 1)
                    eng.wait_ge(s_h[par], 16 * j)
                eng.tensor_scalar(xh[:, par, :], xt[:, par, :], mv[:, par, 0:1], rstd[:, par:par + 1],
                                  ALU.subtract, ALU.mult).then_inc(s_xh, 1)
            mvnil = m.sb("mvnil", [P, 1])
            node_tiles(v, body)
            ch = Chain(v, ch_v)
            v.wait_ge(s_G, NT)
            v.tensor_tensor(lg[:, NT - 1:NT, :], psG[:, 0:X].unsqueeze(1), bgb[:, :].unsqueeze(1), ALU.add).then_inc(s_lg, 1)
            v.wait_ge(s_lg, NT)
            v.wait_ge(s_io, 4)
            t3 = lambda a: a[:, :].unsqueeze(2).to_broadcast([P, NT, X])
            x3 = lambda a: a[:, :].unsqueeze(1).to_broadcast([P, NT, X])
            ch(v.tensor_reduce(top[:, :], lg[:, :, :], AX.X, ALU.max))
            v.tensor_tensor(lg[:, :, :], lg[:, :, :], t3(top), ALU.subtract).then_inc(s_ein, 1)
            v.wait_ge(s_ex, 1)
            ch(v.tensor_reduce(top[:, :], pr[:, :, :], AX.X, ALU.add))
            ch(v.reciprocal(top[:, :], top[:, :]))
            ch(v.tensor_tensor(pr[:, :, :], pr[:, :, :], t3(top), ALU.mult))
            for n in range(2):
                gate = keep["gate"][n]
                ch(v.tensor_reduce(gate[:, :], pr[:, :, :], AX.X, ALU.max))
                ch(v.tensor_tensor(tmp[:, :, :], pr[:, :, :], t3(gate), ALU.is_equal))
                ch(v.tensor_tensor(tmp[:, :, :], tmp[:, :, :], x3(back), ALU.mult))
                ch(v.tensor_reduce(top[:, :], tmp[:, :, :], AX.X, ALU.max))
                ch(v.tensor_tensor(M[n][:, :, :], t3(top), x3(back), ALU.is_equal))
                if n == 0:
                    ch(v.scalar_tensor_tensor(pr[:, :, :], M[0][:, :, :], -2.0, pr[:, :, :], ALU.mult, ALU.add))
            v.tensor_tensor(both[:, :, :], M[0][:, :, :].rearrange("p c e -> p e c"),
                            M[1][:, :, :].rearrange("p c e -> p e c"), ALU.add).then_inc(s_both, 1)
            v.wait_ge(s_rc, 2)
            flat = lambda a: a[:, :, :].rearrange("p b c -> p (b c)")
            ch(v.tensor_tensor_scan(flat(S), flat(T), flat(T), 0.0, ALU.add, ALU.bypass))
            v.tensor_copy(begin[:, 1:X + 1], S[:, :, NT - 1])
            ch(v.memset(begin[:, 0:1], 0.0))
            ch(v.tensor_tensor(nt[:, :], begin[:, 1:X + 1], begin[:, 0:X], ALU.subtract))
            ch(v.tensor_scalar(nt[:, :], nt[:, :], float(P - 1), 1.0 / P, ALU.add, ALU.mult))
            ch(v.tensor_scalar(nt[:, :], nt[:, :], -0.498, ROUND, ALU.add, ALU.add))
            ch(v.tensor_scalar(nt[:, :], nt[:, :], -ROUND, None, ALU.add))
            ch(v.tensor_tensor_scan(ntc[:, :], nt[:, :], nt[:, :], 0.0, ALU.add, ALU.bypass))
            ch(v.tensor_tensor(base[:, :], ntc[:, :], nt[:, :], ALU.subtract))
            ch(v.tensor_scalar(base[:, :], base[:, :], float(P), None, ALU.mult))
            ch(v.tensor_tensor(base[:, :], base[:, :], begin[:, 0:X], ALU.subtract))
            ch(v.tensor_tensor(flat(S), flat(S), flat(T), ALU.subtract))
            ch(v.tensor_tensor(flat(S), flat(S), flat(R), ALU.add))
            ch(v.tensor_tensor(S[:, :, :], S[:, :, :], base[:, :].unsqueeze(2).to_broadcast([P, X, NT]), ALU.add))
            for n in range(2):
                ch(v.tensor_tensor(tmp[:, :, :], M[n][:, :, :], S[:, :, :].rearrange("p e c -> p c e"), ALU.mult))
                ch(v.tensor_reduce(posf[:, :], tmp[:, :, :], AX.X, ALU.add))
                v.tensor_copy(keep["pos"][n][:, :], posf[:, :]).then_inc(s_pos, 1)
            ch(v.tensor_tensor(tc[:, :, :], tj[:, :].unsqueeze(2).to_broadcast([P, TILES, X]),
                               ntc[:, :].unsqueeze(1).to_broadcast([P, TILES, X]), ALU.is_ge))
            ch(v.tensor_reduce(te[:, :], tc[:, :, :], AX.X, ALU.add))
            ch(v.tensor_scalar(te[:, :], te[:, :], float(X - 1), None, ALU.min))
            ch(v.tensor_copy(keep["expert"][:, :], te[:, :]))
    return m


def stage4(nc, k, keep, dram, ins):
    W1, W2 = keep["W1"], keep["W2"]
    HT = TILES // 2
    assert TILES % 2 == 1
    ctx = ExitStack()
    with ctx:
        m = Mem(nc, ctx, "s4")
        b1 = m.sb("b1", [P, X * HID])
        b2 = m.sb("b2", [P, X * D])
        tokr = m.sb("tokr", [P, P], I32)
        tokf = m.sb("tokf", [P, P])
        tok = m.sb("tok", [P, TILES], I32)
        ids = m.sb("ids", [P, 2], I32)
        xg = m.sb("xg", [P, 2, D])
        xT = m.sb("xT", [P, 2, KD, P])
        h = m.sb("h", [P, 2, HID])
        hT = m.sb("hT", [P, 2, KH, P])
        y = m.sb("y", [P, 2, D])
        psT = m.ps("psT", (P, 2, 512))
        psH = m.ps("psH", (P, 2, 512))
        psY = m.ps("psY", (P, 2, 512))
        psHT = m.ps("psHT", (P, 2, 512))

        s_bias = m.sem("s4_biases_loaded")
        s_clear = m.sem("s4_ids_cleared")
        s_tok = m.sem("s4_ids_loaded")
        s_tokf = m.sem("s4_ids_float")
        s_tokT = m.sem("s4_ids_transposed")
        s_toki = m.sem("s4_ids")
        s_ids = m.sem("s4_tile_ids")
        s_xg = [m.sem(f"s4_rows_gathered{i}") for i in range(2)]
        s_T = m.sem("s4_transposed")
        s_Tc = m.sem("s4_transposed_copied")
        s_H = m.sem("s4_hidden_product")
        s_h = m.sem("s4_hidden_biased")
        s_HT = m.sem("s4_hidden_transposed")
        s_hT = m.sem("s4_hidden_relu")
        s_Y = m.sem("s4_output_product")
        s_y = m.sem("s4_output_biased")
        s_yst = [m.sem(f"s4_output_stored{i}") for i in range(2)]
        s_gate = m.sem("s4_gate")

        yv = dram["yrow"].rearrange("(t p) d -> t p d", p=P)

        def tiles(eng, body):
            body(eng, 0, 0)
            body(eng, 0, 1)
            with eng.Fori(1, HT) as j:
                body(eng, j, 0)
                body(eng, j, 1)
            body(eng, HT, 0)

        def expert(eng, i):
            eng.sem_inc(s_gate, 1)
            return eng.value_load(keep["expert"][0:1, bass.ds(i, 1)], min_val=0, max_val=X - 1)

        block = ctx.enter_context(nc.Block())

        @block.sync
        def _(sp):
            sp.wait_ge(s_clear, 1)
            sp.dma_start(tokr[0:TILES, :], dram["slots"].rearrange("(j p) a -> j (p a)", p=P)).then_inc(s_tok, 16)
            sp.dma_start(b1[:, :], row_bcast(ins["b1"], X * HID)).then_inc(s_bias, 16)
            sp.dma_start(b2[:, :], row_bcast(ins["b2"], X * D)).then_inc(s_bias, 16)

            def body(eng, j, par):
                i = 2 * j + par
                eng.wait_ge(s_y, i + 1)
                eng.dma_start(yv[i, :, :], y[:, par, :]).then_inc(s_yst[par], 16)
            tiles(sp, body)
            sp.wait_ge(s_yst[0], 16 * (HT + 1))
            sp.wait_ge(s_yst[1], 16 * HT)

        @block.gpsimd
        def _(g):
            g.wait_ge(s_toki, 1)

            def body(eng, j, par):
                i = 2 * j + par
                after(eng, s_T, i - 1)
                eng.tensor_copy(ids[:, par:par + 1], tok[:, bass.ds(i, 1)]).then_inc(s_ids, 1)
                eng.wait_ge(s_ids, i + 1)
                eng.sem_inc(s_gate, 1)
                eng.indirect_dma_start(xg[:, par, :], None, dram["hrow"],
                                       bass.IndirectOffsetOnAxis(ap=ids[:, par:par + 1], axis=0)).then_inc(s_xg[par], 16)
            tiles(g, body)

        @block.tensor
        def _(t):
            t.wait_ge(s_tokf, 1)
            t.transpose(psT[:, 0, 0:P], tokf[:, :], k["ident"][:, :]).then_inc(s_tokT, 1)
            t.wait_ge(s_toki, 1)
            t.wait_ge(keep["s_W"], 32)

            def rows_T(eng, j, par):
                i = 2 * j + par
                eng.wait_ge(s_xg[par], 16 * (j + 1))
                after(eng, s_Tc, i - 1)
                for c in range(KD):
                    ins_ = eng.transpose(psT[:, par, c * P:(c + 1) * P], xg[:, par, c * P:(c + 1) * P], k["ident"][:, :])
                ins_.then_inc(s_T, 1)

            def hidden(eng, i, par):
                eng.wait_ge(s_Tc, i + 1)
                after(eng, s_h, i - 1)
                e = expert(eng, i)
                for c in range(KD):
                    ins_ = eng.matmul(psH[:, par, 0:HID], xT[:, par, c, :], W1[:, bass.ds(e * KD + c, 1), :].rearrange("p a n -> p (a n)"),
                                      start=c == 0, stop=c == KD - 1)
                ins_.then_inc(s_H, 1)

            def hidden_T(eng, i, par):
                eng.wait_ge(s_h, i + 1)
                after(eng, s_hT, i - 1)
                for c in range(KH):
                    ins_ = eng.transpose(psHT[:, par, c * P:(c + 1) * P], h[:, par, c * P:(c + 1) * P], k["ident"][:, :])
                ins_.then_inc(s_HT, 1)

            def output(eng, i, par):
                eng.wait_ge(s_hT, i + 1)
                after(eng, s_y, i - 1)
                e = expert(eng, i)
                for c in range(KH):
                    ins_ = eng.matmul(psY[:, par, :], hT[:, par, c, :], W2[:, bass.ds(e * KH + c, 1), :].rearrange("p a n -> p (a n)"),
                                      start=c == 0, stop=c == KH - 1)
                ins_.then_inc(s_Y, 1)

            def body(eng, j, par):
                i = 2 * j + par
                hidden(eng, i, par)
                if not (isinstance(j, int) and i == TILES - 1):
                    rows_T(eng, j + par, 1 - par)
                if not (isinstance(j, int) and i == 0):
                    output(eng, i - 1, 1 - par)
                hidden_T(eng, i, par)
            rows_T(t, 0, 0)
            tiles(t, body)
            output(t, TILES - 1, (TILES - 1) % 2)

        @block.scalar
        def _(a):
            def copy_T(eng, i, par):
                eng.wait_ge(s_T, i + 1)
                after(eng, s_H, i - 1)
                eng.activation(xT[:, par, :, :].rearrange("p k n -> p (k n)"), psT[:, par, :], ACT.Copy).then_inc(s_Tc, 1)

            def body(eng, j, par):
                i = 2 * j + par
                if not (isinstance(j, int) and i == TILES - 1):
                    copy_T(eng, i + 1, 1 - par)
                eng.wait_ge(s_HT, i + 1)
                after(eng, s_Y, i - 1)
                eng.activation(hT[:, par, :, :].rearrange("p k n -> p (k n)"), psHT[:, par, 0:HID], ACT.Relu).then_inc(s_hT, 1)
            copy_T(a, 0, 0)
            tiles(a, body)

        @block.vector
        def _(v):
            v.memset(tokr[:, :], 0).then_inc(s_clear, 1)
            v.wait_ge(s_tok, 16)
            v.tensor_copy(tokf[:, :], tokr[:, :]).then_inc(s_tokf, 1)
            v.wait_ge(s_tokT, 1)
            v.tensor_copy(tok[:, :], psT[:, 0, 0:TILES]).then_inc(s_toki, 1)
            v.wait_ge(s_bias, 32)

            def output(eng, i, j, par):
                e = expert(eng, i)
                eng.wait_ge(s_Y, i + 1)
                after(eng, s_yst[par], 16 * j)
                eng.tensor_tensor(y[:, par, :], psY[:, par, :], b2[:, bass.ds(e * D, D)], ALU.add).then_inc(s_y, 1)

            def body(eng, j, par):
                i = 2 * j + par
                e = expert(eng, i)
                eng.wait_ge(s_H, i + 1)
                after(eng, s_HT, i - 1)
                eng.tensor_tensor(h[:, par, :], psH[:, par, 0:HID], b1[:, bass.ds(e * HID, HID)], ALU.add).then_inc(s_h, 1)
                if not (isinstance(j, int) and i == 0):
                    output(eng, i - 1, j + par - 1, 1 - par)
            tiles(v, body)
            output(v, TILES - 1, HT, (TILES - 1) % 2)
    return m


def stage5(nc, k, keep, dram, ins):
    B = 4
    assert NT % B == 1
    ctx = ExitStack()
    with ctx:
        m = Mem(nc, ctx, "s5")
        gam = m.sb("gamma", [P, D])
        bet = m.sb("beta", [P, D])
        pc = m.sb("pc", [P, B, 2], I32)
        y1 = m.sb("y1", [P, B, D])
        y2 = m.sb("y2", [P, B, D])
        hr = m.sb("hr", [P, B, D])
        xr = m.sb("xr", [P, B, D])
        nid = m.sb("nid", [P, B, 4], I32)
        a1 = m.sb("a1", [P, B, D])
        a2 = m.sb("a2", [P, B, D])
        xb = m.sb("xb", [P, B, D])
        nrm = m.sb("nrm", [P, B, D])
        res = m.sb("res", [P, B, D])
        stats = m.sb("stats", [P, B, 6])
        mv = m.sb("mv", [P, B, 2])
        sd = m.sb("sd", [P, B])
        rstd = m.sb("rstd", [P, B])

        s_gb = m.sem("s5_gamma_beta_loaded")
        s_in = [m.sem(f"s5_rows_loaded{i}") for i in range(B)]
        s_y = [m.sem(f"s5_choices_gathered{i}") for i in range(B)]
        s_pc = m.sem("s5_places")
        s_a1 = m.sem("s5_first_choice")
        s_a2 = m.sem("s5_both_choices")
        s_bn = m.sem("s5_stats")
        s_mv = m.sem("s5_mean_var")
        s_sd = m.sem("s5_std")
        s_rs = m.sem("s5_rstd")
        s_g = m.sem("s5_centred_times_gamma")
        s_xb = m.sem("s5_residual_plus_beta")
        s_r = m.sem("s5_results")
        s_out = [m.sem(f"s5_results_stored{i}") for i in range(B)]
        s_gate = m.sem("s5_gate")
        tile_of = lambda name, i: dram[name].rearrange("(t p) d -> t p d", p=P)[i, :, :]

        def steps(eng, body):
            for q in range(B):
                body(q, 0, q)
            with eng.Fori(1, NT // B) as j:
                for q in range(B):
                    body(B * j + q, j, q)
            body(NT - 1, NT // B, 0)

        block = ctx.enter_context(nc.Block())

        @block.sync
        def _(sp):
            sp.dma_start(gam[:, :], row_bcast(ins["gamma"], D)).then_inc(s_gb, 16)
            sp.dma_start(bet[:, :], row_bcast(ins["beta"], D)).then_inc(s_gb, 16)

            def body(i, j, q):
                after(sp, s_r, i - B + 1)
                sp.sem_inc(s_gate, 1)
                after(sp, s_out[q], 16 * j)
                sp.dma_start(hr[:, q, :], tile_of("hrow", i)).then_inc(s_in[q], 16)
                sp.dma_start(xr[:, q, :], tile_of("xnew", i)).then_inc(s_in[q], 16)
                sp.dma_start(nid[:, q, :], tile_of("order", i)).then_inc(s_in[q], 16)
            steps(sp, body)

        @block.gpsimd
        def _(g):
            def scatter(i, j, q):
                g.wait_ge(s_r, i + 1)
                g.wait_ge(s_in[q], 48 * (j + 1))
                g.sem_inc(s_gate, 1)
                g.indirect_dma_start(dram["out"], bass.IndirectOffsetOnAxis(ap=nid[:, q, 0:1], axis=0),
                                     res[:, q, :], None).then_inc(s_out[q], 16)

            def body(i, j, q):
                after(g, s_a2, i - B + 1)
                for n in range(2):
                    ins_ = g.tensor_copy(pc[:, q, n:n + 1], keep["pos"][n][:, bass.ds(i, 1)])
                ins_.then_inc(s_pc, 1)
                g.wait_ge(s_pc, i + 1)
                g.sem_inc(s_gate, 1)
                for n, y in enumerate((y1, y2)):
                    g.indirect_dma_start(y[:, q, :], None, dram["yrow"],
                                         bass.IndirectOffsetOnAxis(ap=pc[:, q, n:n + 1], axis=0)).then_inc(s_y[q], 16)
                if not (isinstance(i, int) and i < 2):
                    scatter(i - 2, j if q >= 2 else j - 1, (q - 2) % B)
            steps(g, body)
            scatter(NT - 2, NT // B - 1, B - 1)
            scatter(NT - 1, NT // B, 0)
            for q in range(B):
                g.wait_ge(s_out[q], 16 * (NT // B + (q == 0)))

        @block.scalar
        def _(a):
            def body(i, j, q):
                a.wait_ge(s_mv, i + 1)
                after(a, s_rs, i - B + 1)
                a.activation(sd[:, q:q + 1], mv[:, q, 1:2], ACT.Sqrt, bias=k["eps"][:, 0:1]).then_inc(s_sd, 1)
            steps(a, body)

        @block.vector
        def _(v):
            v.wait_ge(s_gb, 32)

            def body(i, j, q):
                g1, g2 = (keep["gate"][n][:, bass.ds(i, 1)] for n in range(2))
                before = not (isinstance(i, int) and i == 0)
                jp, qp = (j, q - 1) if q else (j - 1, B - 1)
                v.wait_ge(s_y[q], 32 * (j + 1))
                v.wait_ge(s_in[q], 48 * (j + 1))
                v.scalar_tensor_tensor(a1[:, q, :], y1[:, q, :], g1, hr[:, q, :], ALU.mult, ALU.add).then_inc(s_a1, 1)
                if before:
                    v.wait_ge(s_sd, i)
                    v.reciprocal(rstd[:, qp:qp + 1], sd[:, qp:qp + 1]).then_inc(s_rs, 1)
                v.tensor_tensor(xb[:, q, :], xr[:, q, :], bet[:, :], ALU.add).then_inc(s_xb, 1)
                v.wait_ge(s_a1, i + 1)
                v.scalar_tensor_tensor(a2[:, q, :], y2[:, q, :], g2, a1[:, q, :], ALU.mult, ALU.add).then_inc(s_a2, 1)
                if before:
                    centre(i - 1, qp)
                v.wait_ge(s_a2, i + 1)
                v.bn_stats(stats[:, q, :], a2[:, q, :]).then_inc(s_bn, 1)
                if before:
                    result(i - 1, jp, qp)
                v.wait_ge(s_bn, i + 1)
                v.tensor_copy(nil[:, 0:1], stats[:, q, 0:1])
                v.bn_aggr(mv[:, q, :], stats[:, q, :]).then_inc(s_mv, 1)

            def centre(i, q):
                v.wait_ge(s_mv, i + 1)
                v.scalar_tensor_tensor(nrm[:, q, :], a2[:, q, :], mv[:, q, 0:1], gam[:, :], ALU.subtract, ALU.mult).then_inc(s_g, 1)

            def result(i, j, q):
                v.wait_ge(s_g, i + 1)
                v.wait_ge(s_rs, i + 1)
                v.wait_ge(s_xb, i + 1)
                after(v, s_out[q], 16 * j)
                v.scalar_tensor_tensor(res[:, q, :], nrm[:, q, :], rstd[:, q:q + 1], xb[:, q, :], ALU.mult, ALU.add).then_inc(s_r, 1)
            nil = m.sb("nil", [P, 1])
            steps(v, body)
            v.wait_ge(s_sd, NT)
            v.reciprocal(rstd[:, 0:1], sd[:, 0:1]).then_inc(s_rs, 1)
            centre(NT - 1, 0)
            result(NT - 1, NT // B, 0)


def build(nc, a, out):
    dram = {"out": out}
    for name, shape, dt in (("rowL", (NP, ROW), F32), ("rowR", (NP, ROW), F32), ("rowX", (NP, D), F32), ("order", (NP, 4), I32),
                            ("units", (UC * P, 4), I32), ("xnew", (NP, D), F32), ("hrow", (NP, D), F32),
                            ("slots", (TILES * P, 1), I32), ("yrow", (TILES * P, D), F32)):
        dram[name] = nc.dram_tensor(f"tmp_{name}", shape, dt).ap()
    ctx = ExitStack()
    with ctx:
        m = Mem(nc, ctx, "all")
        k = constants(nc, m)
        keep = {"rounds": m.sb("rounds", [1, 1], I32),
                "pos": [m.sb(f"pos{n}", [P, NT], I32) for n in range(2)],
                "gate": [m.sb(f"gate{n}", [P, NT]) for n in range(2)],
                "expert": m.sb("expert", [P, TILES], I32),
                "s_W": m.sem("expert_weights_loaded")}
        graph = ExitStack()
        with graph:
            g = Mem(nc, graph, "graph")
            keep["att"] = g.sb("att_pos", [P, D])
            count = ExitStack()
            with count:
                keep["psC"] = Mem(nc, count, "count").ps("psC")
                stage1(nc, k, keep, dram, a).give_back()
                stage1b(nc, k, keep, dram).give_back()
            stage2(nc, k, keep, dram, a).give_back()
        experts = ExitStack()
        with experts:
            x = Mem(nc, experts, "experts")
            keep["W1"] = x.sb("W1", [P, X * KD, HID])
            keep["W2"] = x.sb("W2", [P, X * KH, D])
            stage3(nc, k, keep, dram, a).give_back()
            stage4(nc, k, keep, dram, a).give_back()
        stage5(nc, k, keep, dram, a)


def kernel(x, src, dst, L0_gnn_W_l, L0_gnn_W_r, L0_gnn_att, L0_gnn_bias, L0_ffn_Wg, L0_ffn_bg, L0_ffn_W1,
           L0_ffn_b1, L0_ffn_W2, L0_ffn_b2, L0_ffn_gamma, L0_ffn_beta):
    import concourse.bacc as bacc
    import numpy as np
    from concourse.bass_utils import run_bass_kernel_spmd

    def padded(a, n, fill):
        a = np.asarray(a)
        return np.concatenate([a, np.full((n - a.shape[0],) + a.shape[1:], fill, a.dtype)])

    arrays = {
        "x": padded(x, NP, 0),
        "src": padded(src, E + P, 0).reshape(1, -1),
        "dst": padded(dst, EP, NT * P + P),
        "W_l": L0_gnn_W_l, "W_r": L0_gnn_W_r, "att": np.reshape(L0_gnn_att, -1), "bias": L0_gnn_bias,
        "Wg": L0_ffn_Wg, "bg": L0_ffn_bg, "W1": L0_ffn_W1, "b1": np.reshape(L0_ffn_b1, -1),
        "W2": L0_ffn_W2, "b2": np.reshape(L0_ffn_b2, -1), "gamma": L0_ffn_gamma, "beta": L0_ffn_beta,
    }
    arrays = {f"in_{n}": np.ascontiguousarray(v) for n, v in arrays.items()}
    nc = bacc.Bacc("TRN2", target_bir_lowering=False, num_devices=1)
    a = {n[3:]: nc.dram_tensor(n, v.shape, mybir.dt.from_np(v.dtype), kind="ExternalInput").ap() for n, v in arrays.items()}
    out = nc.dram_tensor("out_rows", (NP, D), F32, kind="ExternalOutput").ap()
    build(nc, a, out)
    r = run_bass_kernel_spmd(nc, [arrays], core_ids=[0])
    return r.results[0]["out_rows"][:N]
```
